# Optimizing a Trainium2 kernel written in Bass

```python
import numpy as np
import jax
import jax.numpy as jnp

def _softmax(x, axis=-1):
    return jax.nn.softmax(x, axis=axis)
def _gelu(x):
    return jax.nn.gelu(x, approximate=True)
def _silu(x):
    return jax.nn.silu(x)
def _sigmoid(x):
    return jax.nn.sigmoid(x)
def _layernorm(x, axis=-1, eps=1e-5):
    m = jnp.mean(x, axis=axis, keepdims=True)
    v = jnp.var(x, axis=axis, keepdims=True)
    return (x - m) / jnp.sqrt(v + eps)
def _scatter_add(tgt, idx, src, axis=0):
    return tgt.at[idx].add(src)
def _segment_sum(src, seg, n):
    return jax.ops.segment_sum(src, seg, n)

kernel_name = 'mk_adj_preln_d4_adj_512_fc15c1'

def setup_inputs(seed: int = 0):
    np.random.seed(seed)
    _w = jnp.asarray
    def _rec_inputs():
        import jax
        import jax.numpy as jnp
        _gk = jax.random.key(seed)
        x = 7.22e-05 + 1 * jax.random.normal(jax.random.fold_in(_gk, 1), (64, 256, 512), jnp.float32)
        _a = jax.random.bernoulli(jax.random.fold_in(_gk, 2), 0.125, (64, 256, 256))
        _a = jnp.logical_or(_a, jnp.swapaxes(_a, -1, -2))
        _a = jnp.logical_or(_a, jnp.eye(256, dtype=bool))
        _af = _a.astype(jnp.float32)
        _af = _af * jax.random.uniform(jax.random.fold_in(_gk, 3), (64, 256, 256), jnp.float32, 0.05, 1)
        adj = _af
        return x, adj
    x, adj = _rec_inputs()
    def _L0_gnn_setup():
        import jax, jax.numpy as jnp
        import numpy as np
        IN_F = 512
        OUT_F = 512
        ALPHA = 0.2
        NEG_INF = -9000000000000000.0
        key = jax.random.key(seed)
        k1, k2, k3, k4 = jax.random.split(key, 4)
        B, S = (8, 2048)
        hidden_state = jax.random.normal(k1, (B, S, IN_F), dtype=jnp.float32)
        adjacent_matrix = jax.random.uniform(k2, (B, S, S), dtype=jnp.float32)
        bound = 1.0 / np.sqrt(IN_F)
        W = jax.random.uniform(k3, (IN_F, OUT_F), dtype=jnp.float32, minval=-bound, maxval=bound)
        a_bound = 1.414 * np.sqrt(6.0 / (2 * OUT_F + 1))
        a = jax.random.uniform(k4, (2 * OUT_F, 1), dtype=jnp.float32, minval=-a_bound, maxval=a_bound)
        return {'hidden_state': hidden_state, 'adjacent_matrix': adjacent_matrix, 'W': W, 'a': a}
    _L0_gnn_all = _L0_gnn_setup()
    _L0_gnn_in = {k: v for k, v in _L0_gnn_all.items() if k in ('W', 'a', )}
    del _L0_gnn_all

    def _L1_gnn_setup():
        import jax, jax.numpy as jnp
        import numpy as np
        N = 8192
        F = 512
        C = 512
        key = jax.random.key(seed)
        k1, k2, k3 = jax.random.split(key, 3)
        X = jax.random.normal(k1, (1, N, F), dtype=jnp.float32)
        A = jax.random.uniform(k2, (1, N, N), dtype=jnp.float32)
        kernel = jax.random.normal(k3, (F, C), dtype=jnp.float32) * (1.0 / np.sqrt(F))
        bias = jnp.zeros((C,), dtype=jnp.float32)
        return {'X': X, 'A': A, 'kernel': kernel, 'bias': bias}
    _L1_gnn_all = _L1_gnn_setup()
    _L1_gnn_in = {k: v for k, v in _L1_gnn_all.items() if k in ('kernel', 'bias', )}
    del _L1_gnn_all

    def _L2_gnn_setup():
        import jax, jax.numpy as jnp
        import numpy as np
        key = jax.random.key(seed)
        k1, k2, k3 = jax.random.split(key, 3)
        B, N, F, D = (8, 2048, 512, 512)
        x = jax.random.normal(k1, (B, N, F), dtype=jnp.float32)
        a = jax.random.uniform(k2, (B, N, N), dtype=jnp.float32)
        kernel = jax.random.normal(k3, (F, D), dtype=jnp.float32) * (1.0 / np.sqrt(F))
        return {'x': x, 'a': a, 'kernel': kernel}
    _L2_gnn_all = _L2_gnn_setup()
    _L2_gnn_in = {k: v for k, v in _L2_gnn_all.items() if k in ('kernel', )}
    del _L2_gnn_all

    def _L3_gnn_setup():
        import jax, jax.numpy as jnp
        import numpy as np
        EPS = 1e-06
        key = jax.random.key(seed)
        k1, k2, k3 = jax.random.split(key, 3)
        B, N, F, O = (8, 4096, 512, 512)
        x = jax.random.normal(k1, (B, N, F), dtype=jnp.float32)
        adj = jax.random.uniform(k2, (B, N, N), dtype=jnp.float32)
        W = jax.random.normal(k3, (O, 2 * F), dtype=jnp.float32) * (1.0 / np.sqrt(2 * F))
        return {'x': x, 'adj': adj, 'W': W}
    _L3_gnn_all = _L3_gnn_setup()
    _L3_gnn_in = {k: v for k, v in _L3_gnn_all.items() if k in ('W', )}
    del _L3_gnn_all

    return {
        "x": x,
        "adj": adj,
        "L0_gnn_W": _L0_gnn_in["W"],
        "L0_gnn_a": _L0_gnn_in["a"],
        "L1_gnn_kernel": _L1_gnn_in["kernel"],
        "L1_gnn_bias": _L1_gnn_in["bias"],
        "L2_gnn_kernel": _L2_gnn_in["kernel"],
        "L3_gnn_W": _L3_gnn_in["W"],
    }

def reference(x, adj, L0_gnn_W, L0_gnn_a, L1_gnn_kernel, L1_gnn_bias, L2_gnn_kernel, L3_gnn_W):
    import jax
    import jax.numpy as jnp
    def _L0_gnn_ref(hidden_state, adjacent_matrix, W, a):
        import jax, jax.numpy as jnp
        import numpy as np
        IN_F = 512
        OUT_F = 512
        ALPHA = 0.2
        NEG_INF = -9000000000000000.0
        Wh = jnp.einsum('bsi,io->bso', hidden_state, W)
        Wh1 = Wh @ a[:OUT_F, :]
        Wh2 = Wh @ a[OUT_F:, :]
        e = Wh1 + jnp.swapaxes(Wh2, 1, 2)
        e = jax.nn.leaky_relu(e, negative_slope=ALPHA)
        attention = jnp.where(adjacent_matrix > 0.5, e, NEG_INF)
        attention = jax.nn.softmax(attention, axis=1)
        h_prime = jnp.einsum('bst,bto->bso', attention, Wh)
        return jax.nn.elu(h_prime)

    def _L1_gnn_ref(X, A, kernel, bias):
        import jax, jax.numpy as jnp
        import numpy as np
        N = 8192
        F = 512
        C = 512
        Ah = A + jnp.eye(A.shape[-1], dtype=A.dtype)[None, :, :]
        dh = jax.lax.rsqrt(jnp.sum(Ah, axis=-1))
        An = dh[:, :, None] * Ah * dh[:, None, :]
        out = jnp.einsum('bnm,bmf,fc->bnc', An, X, kernel) + bias
        return jax.nn.relu(out)

    def _L2_gnn_ref(x, a, kernel):
        import jax, jax.numpy as jnp
        import numpy as np
        t = jnp.einsum('bnm,bmf->bnf', a, x)
        out = jnp.einsum('bnf,fd->bnd', t, kernel)
        out = jax.nn.relu(out)
        mask = (jnp.sum((x != 0).astype(jnp.float32), axis=-1, keepdims=True) > 0).astype(jnp.float32)
        return out * mask

    def _L3_gnn_ref(x, adj, W):
        import jax, jax.numpy as jnp
        import numpy as np
        EPS = 1e-06
        deg = jnp.sum(adj, axis=-1, keepdims=True)
        agg = jnp.einsum('bij,bjf->bif', adj, x) / jnp.maximum(deg, EPS)
        cat = jnp.concatenate([x, agg], axis=2)
        out = jnp.einsum('bnf,of->bno', cat, W)
        return jax.nn.relu(out)

    h = jnp.maximum(_layernorm(x, axis=-1), 0.0)
    x = x + _L0_gnn_ref(h, adj, L0_gnn_W, L0_gnn_a)
    h = jnp.maximum(_layernorm(x, axis=-1), 0.0)
    x = x + _L1_gnn_ref(h, adj, L1_gnn_kernel, L1_gnn_bias)
    h = jnp.maximum(_layernorm(x, axis=-1), 0.0)
    x = x + _L2_gnn_ref(h, adj, L2_gnn_kernel)
    h = jnp.maximum(_layernorm(x, axis=-1), 0.0)
    x = x + _L3_gnn_ref(h, adj, L3_gnn_W)
    return x


_drawn_inputs = setup_inputs


def setup_inputs(seed=0):
    import zlib

    import numpy as np

    out = dict(_drawn_inputs(seed))
    spreads = {'L1_gnn_bias': (0.0, 0.1)}
    factors = {'L0_gnn_a': 3.369}
    for name, (base, spread) in spreads.items():
        noise = np.random.default_rng([zlib.crc32(name.encode()), seed]).standard_normal(out[name].shape)
        drawn = base * np.exp(spread * noise) if base else spread * noise
        out[name] = jnp.asarray(drawn.astype(out[name].dtype))
    for name, factor in factors.items():
        out[name] = (out[name] * factor).astype(out[name].dtype)
    return out
```

```python
from contextlib import ExitStack

import concourse.bass as bass
from concourse import mybir

F32 = mybir.dt.float32
F32R = mybir.dt.float32r
ALU = mybir.AluOpType
ACT = mybir.ActivationFunctionType
AX = mybir.AxisListType

P = 128
LAYERS = 4
STREAMS = 4
MASKED = -9000000000000000.0
SLOPE = 0.2
LN_EPS = 1e-5
DEG_EPS = 1e-6


class Schedule:

    def __init__(self, graphs):
        self.graphs = graphs
        self.turns = graphs // STREAMS
        self.rounds = LAYERS * self.turns + STREAMS - 1
        self.steps = STREAMS * self.rounds
        self.span = STREAMS * LAYERS
        self.first, self.last = -3, self.steps
        self.loop_at = self.span + STREAMS
        whole = next(k for k in range(self.span, self.steps) if not self.valid(k))
        self.loops = (whole - 3 - self.loop_at) // self.span

    def valid(self, k):
        s, r = k % STREAMS, k // STREAMS
        return 0 <= k < self.steps and 0 <= r - s < LAYERS * self.turns

    def layer(self, k):
        return (k // STREAMS - k % STREAMS) % LAYERS if self.valid(k) else None

    def graph(self, k):
        s, r = k % STREAMS, k // STREAMS
        return STREAMS * ((r - s) // LAYERS) + s

    def count(self, k, layers=range(LAYERS)):
        return sum(self.layer(i) in layers for i in range(k + 1) if self.valid(i))


class Step:

    def __init__(self, plan, k, turn):
        self.plan, self.k, self.turn = plan, k, turn
        self.valid, self.layer = plan.valid(k), plan.layer(k)
        self.stream = k % STREAMS
        self.odd = k % 2
        self.g0 = plan.graph(k) if self.valid else None

    def affine(self, value_at):
        base = value_at(self.k)
        if self.turn is None:
            return base
        slope = value_at(self.k + self.plan.span) - base
        for i in range(self.plan.loops):
            assert value_at(self.k + i * self.plan.span) == base + slope * i
        assert base > 0 or slope == 0, "a wait below one in the loop's first turn"
        return base + slope * self.turn if slope else base

    def graph(self, ahead=0):
        g = self.g0 + ahead
        return g if self.turn is None else g + STREAMS * self.turn

    def done(self, back=0, layers=range(LAYERS), per=1, part=None):
        def value_at(k):
            k -= back
            if part is None:
                return per * self.plan.count(k, layers)
            return per * self.plan.count(k - 1, layers) + (part + 1 if self.plan.layer(k) in layers else 0)
        return self.affine(value_at)

    def done_by_last(self, layer, per=1):
        def value_at(k):
            before = [i for i in range(k) if self.plan.layer(i) == layer]
            return per * self.plan.count(before[-1]) if before else 0
        return self.affine(value_at)


def gnn_kernel(nc, x, adj, adj_t, w_all, w0_t, a_cols, bias, out):
    G, N, F = x.shape
    NT = N // P
    FT = F // P
    HALF = FT // NT
    plan = Schedule(G)
    L0, L1, L2, L3 = (0,), (1,), (2,), (3,)
    NW = 5
    DOTS = 2 * NT

    with ExitStack() as ctx:
        def sb(name, shape, dt=F32):
            return ctx.enter_context(nc.sbuf_tensor(name, shape, dt))

        def sem(name):
            return ctx.enter_context(nc.semaphore(name))

        w_hi = sb("w_hi", [P, NW, FT, F], F32R)
        w_lo = sb("w_lo", [P, NW, FT, F], F32R)
        v_rows = sb("v_rows", [P, 2, F])
        bias_rows = sb("bias_rows", [P, F])
        ident = sb("ident", [P, P])
        minus_half, ones, ln_eps, minus_one = (sb(n, [P, NT]) for n in ("minus_half", "ones", "ln_eps", "minus_one"))
        carrier = sb("carrier", [P, 1])
        a_sb = sb("a_sb", [P, 2, FT])
        xs = sb("xs", [P, STREAMS, NT, F])
        a_raw = sb("a_raw", [P, STREAMS, NT, N])
        a_hi = sb("a_hi", [P, STREAMS, NT, N], F32R)
        a_lo = sb("a_lo", [P, STREAMS, NT, N], F32R)
        deg = sb("deg", [P, STREAMS, NT])
        deg_one = sb("deg_one", [P, STREAMS, NT])
        deg_rsqrt = sb("deg_rsqrt", [P, STREAMS, NT])
        deg_floor = sb("deg_floor", [P, STREAMS, NT])
        deg_recip = sb("deg_recip", [P, STREAMS, NT])
        x_in = sb("x_in", [P, 2, NT, F])
        a_rows = sb("a_rows", [P, NT, N])
        a_diag = sb("a_diag", [P, NT, P])
        h = sb("h", [P, 2, NT, F])
        h_hi = sb("h_hi", [P, 2, NT, F], F32R)
        h_lo = sb("h_lo", [P, 2, NT, F], F32R)
        t_hi = sb("t_hi", [P, 2, FT, N], F32R)
        t_lo = sb("t_lo", [P, 2, FT, N], F32R)
        t_mean = sb("t_mean", [P, FT, N])
        ht_hi = sb("ht_hi", [P, FT, N], F32R)
        ht_lo = sb("ht_lo", [P, FT, N], F32R)
        recip_rows = sb("recip_rows", [P, N])
        act_out = sb("act_out", [P, 2, NT, F])
        scores = sb("scores", [P, NT, N])
        mask_add = sb("mask_add", [P, NT, N])
        p_hi = sb("p_hi", [P, NT, N], F32R)
        p_lo = sb("p_lo", [P, NT, N], F32R)
        ln_stats = sb("ln_stats", [P, 2, NT, 6])
        ln_mv = sb("ln_mv", [P, 2, NT, 2])
        ln_var = sb("ln_var", [P, 2, NT])
        ln_rstd = sb("ln_rstd", [P, 2, NT])
        ln_scale = sb("ln_scale", [P, 2, NT])
        ln_ms = sb("ln_ms", [P, 2, NT])
        ln_bias = sb("ln_bias", [P, 2, NT])
        h_sum = sb("h_sum", [P, STREAMS, NT])
        row_mask = sb("row_mask", [P, STREAMS, NT])
        wh = sb("wh", [P, 2, 2, NT])
        s_neg = sb("s_neg", [P, NT])
        s_sum = sb("s_sum", [P, NT])
        s_rec = sb("s_rec", [P, NT])

        T = ctx.enter_context(nc.psum_tensor("T", [P, FT, N], F32))
        O = ctx.enter_context(nc.psum_tensor("O", [P, 2, NT, F], F32))
        X = ctx.enter_context(nc.psum_tensor("X", [P, 2, F], F32))
        wh_rows = X[:, 0, 0:N]
        recip_psum = X[:, 0, 0:N]

        stage = [xs[:, NT * b:NT * b + NT].rearrange("p s n f -> p (s n) f") for b in range(2)]

        stage_in = [sem(f"stage_in{b}") for b in range(2)]
        consts_in = sem("consts_in")
        x_loaded = [sem(f"x_loaded{b}") for b in range(2)]
        a_loaded = [sem(f"a_loaded{s}") for s in range(STREAMS)]
        rows_loaded = sem("rows_loaded")
        out_stored = [sem(f"out_stored{b}") for b in range(2)]
        w_hi_ready, w_lo_ready = sem("w_hi_ready"), sem("w_lo_ready")
        v_psum_ready, v_ready = sem("v_psum_ready"), sem("v_ready")
        ident_zero, ident_ready, columns_ready = sem("ident_zero"), sem("ident_ready"), sem("columns_ready")
        t_ready, o_ready = sem("t_ready"), sem("o_ready")
        wh_rows_ready, recip_psum_ready, ht_psum_ready = sem("wh_rows_ready"), sem("recip_psum_ready"), sem("ht_psum_ready")
        stats_ready, mv_ready, ln_part, ln_scaled, ln_ready = (
            sem("stats_ready"), sem("mv_ready"), sem("ln_part"), sem("ln_scaled"), sem("ln_ready"))
        h_ready, h_hi_ready, h_lo_ready, row_mask_ready = (
            sem("h_ready"), sem("h_hi_ready"), sem("h_lo_ready"), sem("row_mask_ready"))
        deg_ready, deg_one_ready, deg_rsqrt_ready, deg_floor_ready, deg_recip_ready = (
            sem("deg_ready"), sem("deg_one_ready"), sem("deg_rsqrt_ready"), sem("deg_floor_ready"), sem("deg_recip_ready"))
        diag_ready, ah_hi_ready, ah_lo_ready, a_hi_ready, a_lo_ready = (
            sem("diag_ready"), sem("ah_hi_ready"), sem("ah_lo_ready"), sem("a_hi_ready"), sem("a_lo_ready"))
        wh_ready, mask_ready, scores_ready, masked_ready, neg_ready, exp_ready, s_rec_ready, p_hi_ready, p_lo_ready = (
            sem("wh_ready"), sem("mask_ready"), sem("scores_ready"), sem("masked_ready"), sem("neg_ready"),
            sem("exp_ready"), sem("s_rec_ready"), sem("p_hi_ready"), sem("p_lo_ready"))
        t_hi_ready, t_lo_ready, t_mean_ready, recip_rows_ready, ht_hi_ready, ht_lo_ready = (
            sem("t_hi_ready"), sem("t_lo_ready"), sem("t_mean_ready"), sem("recip_rows_ready"),
            sem("ht_hi_ready"), sem("ht_lo_ready"))
        exp_out_ready, elu_neg_ready, affine_ready, relu_ready, dve_finished, elu_ready = (
            sem("exp_out_ready"), sem("elu_neg_ready"), sem("affine_ready"), sem("relu_ready"),
            sem("dve_finished"), sem("elu_ready"))

        def periods(eng):
            for j in range(plan.first, plan.loop_at):
                yield lambda k, j=j: Step(plan, j + k, None)
            with eng.Fori(0, plan.loops) as turn:
                for j in range(plan.loop_at, plan.loop_at + plan.span):
                    yield lambda k, j=j: Step(plan, j + k, turn)
            for j in range(plan.loop_at + plan.span * plan.loops, plan.last + 2):
                yield lambda k, j=j: Step(plan, j + k, None)

        def wait(eng, semaphore, value):
            if isinstance(value, int) and value <= 0:
                return
            eng.wait_ge(semaphore, value)

        def tiles(dram, g):
            return dram[g].rearrange("(m p) f -> p m f", p=P)

        def graph_turn(step, every, ahead=0):
            return step.affine(lambda k: 16 * ((plan.graph(k) + ahead) // every + 1))

        def free_act_out(eng, k):
            wait(eng, elu_ready, k.done(2, layers=L0, per=NT))
            wait(eng, dve_finished, k.done(2, per=NT))
            wait(eng, out_stored[k.odd], k.affine(lambda i: 16 * sum(
                plan.layer(e) == 3 for e in range(i - 1) if e % 2 == i % 2)))

        block = ctx.enter_context(nc.Block())

        @block.sync
        def _(sp):
            w_tiles = [w_all[i].rearrange("(c p) n -> p c n", p=P) for i in range(NW)]
            order = [w0_t.rearrange("(c p) n -> p c n", p=P)] + w_tiles
            sp.dma_start(a_sb[:], a_cols).then_inc(consts_in, 16)
            sp.dma_start(bias_rows[:], bias.partition_broadcast(P)).then_inc(consts_in, 16)
            for n, source in enumerate(order):
                if n == 2:
                    sp.wait_ge(v_psum_ready, 1)
                    for g in range(2):
                        sp.dma_start(x_in[:, g], tiles(x, g)).then_inc(x_loaded[g], 16)
                        sp.dma_start(a_raw[:, g], tiles(adj_t, g)).then_inc(a_loaded[g], 16)
                    sp.dma_start(a_rows[:], tiles(adj, 0)).then_inc(rows_loaded, 16)
                elif n > 2:
                    sp.wait_ge(w_lo_ready, n - 2)
                sp.dma_start(stage[n % 2], source).then_inc(stage_in[n % 2], 16)
            for s in range(2, STREAMS):
                sp.dma_start(a_raw[:, s], tiles(adj_t, s)).then_inc(a_loaded[s], 16)

            for step in periods(sp):
                done = step(-1)
                if done.layer == 3:
                    sp.wait_ge(dve_finished, done.done(per=NT))
                    sp.dma_start(tiles(out, done.graph()), act_out[:, done.odd]).then_inc(out_stored[done.stream % 2], 16)
                if done.layer == 0 and done.g0 + 2 < G:
                    sp.wait_ge(dve_finished, done.done(per=NT))
                    sp.dma_start(x_in[:, done.stream % 2], tiles(x, done.graph(2))).then_inc(x_loaded[done.stream % 2], 16)
                att = step(2)
                if att.layer == 0 and att.g0 + 1 < G:
                    sp.wait_ge(deg_ready, att.done(layers=L0))
                    sp.dma_start(a_rows[:], tiles(adj, att.graph(1))).then_inc(rows_loaded, 16)
                pre = step(3)
                if pre.layer == 2 and pre.g0 + STREAMS < G:
                    sp.wait_ge(a_lo_ready, pre.done(layers=L2))
                    sp.dma_start(a_raw[:, pre.stream], tiles(adj_t, pre.graph(STREAMS))).then_inc(a_loaded[pre.stream], 16)
            for b in range(2):
                sp.wait_ge(out_stored[b], 16 * (G // 2))

        @block.tensor
        def _(pe):
            def product(psum, pairs):
                last = None
                for n, (s_hi, s_lo, m_hi, m_lo) in enumerate(pairs):
                    for i, (s, m) in enumerate(((s_hi, m_hi), (s_hi, m_lo), (s_lo, m_hi))):
                        last = nc.tensor.matmul(psum, s, m, start=(n == 0 and i == 0),
                                                stop=(n == len(pairs) - 1 and i == 2))
                return last

            pe.wait_ge(consts_in, 32)
            pe.wait_ge(stage_in[0], 16)
            for v in range(2):
                for c in range(FT):
                    last = nc.tensor.matmul(X[:, v], a_sb[:, v, c:c + 1].to_broadcast([P, P]), stage[0][:, c],
                                            start=(c == 0), stop=(c == FT - 1))
            last.then_inc(v_psum_ready, 1)
            pe.wait_ge(ident_ready, 1)
            pe.wait_ge(v_ready, 1)
            pe.wait_ge(w_hi_ready, NW)
            pe.wait_ge(w_lo_ready, NW)

            def transpose_h(k, half):
                for f in range(HALF * half, HALF * half + HALF):
                    for m in range(NT):
                        c = (f % HALF) * N + m * P
                        last = nc.tensor.transpose(X[:, 1 - half, c:c + P], h[:, k.odd, m, f * P:f * P + P], ident[:])
                last.then_inc(ht_psum_ready, 1)

            def gather(k):
                if k.layer == 3:
                    wait(pe, deg_recip_ready, k.done(layers=L0))
                    wait(pe, scores_ready, k.done(layers=L0, per=NT))
                    wait(pe, ht_lo_ready, k.done(1, layers=L3, per=2))
                    for m in range(NT):
                        last = nc.tensor.transpose(recip_psum[:, m * P:m * P + P],
                                                   deg_recip[:, k.stream, m:m + 1].to_broadcast([P, P]), ident[:])
                    last.then_inc(recip_psum_ready, 1)
                    wait(pe, h_ready, k.done(per=NT))
                    transpose_h(k, 0)
                wait(pe, h_hi_ready, k.done(per=NT))
                wait(pe, h_lo_ready, k.done(per=NT))
                if k.layer == 0:
                    wait(pe, p_lo_ready, k.done(layers=L0, per=NT))
                    m_hi, m_lo = p_hi, p_lo
                else:
                    m_hi, m_lo = a_hi[:, k.stream], a_lo[:, k.stream]
                if k.layer == 1:
                    wait(pe, ah_hi_ready, k.done(layers=L1, per=2))
                    wait(pe, ah_lo_ready, k.done(layers=L1, per=2))
                if k.layer == 2:
                    wait(pe, a_hi_ready, k.done(layers=L2))
                    wait(pe, a_lo_ready, k.done(layers=L2))
                for b in range(2):
                    wait(pe, t_lo_ready, k.done(1, per=2, part=b))
                    for f in range(HALF * b, HALF * b + HALF):
                        c = slice(f * P, f * P + P)
                        last = product(T[:, f], [(h_hi[:, k.odd, m, c], h_lo[:, k.odd, m, c], m_hi[:, m], m_lo[:, m])
                                                 for m in range(NT)])
                    last.then_inc(t_ready, 1)
                if k.layer == 3:
                    wait(pe, recip_rows_ready, k.done(layers=L3))
                    transpose_h(k, 1)

            def spread_scores(k):
                wait(pe, wh_ready, k.done(layers=L0, per=DOTS))
                wait(pe, scores_ready, k.done(1, layers=L0, per=NT))
                wait(pe, ht_lo_ready, k.done(1, layers=L3, per=2))
                for m in range(NT):
                    last = nc.tensor.transpose(wh_rows[:, m * P:m * P + P],
                                               wh[:, k.g0 % 2, 0, m:m + 1].to_broadcast([P, P]), ident[:])
                last.then_inc(wh_rows_ready, 1)

            def project(k):
                for n in range(NT):
                    c = slice(n * P, n * P + P)
                    wait(pe, dve_finished, k.done(2, per=NT, part=n))
                    pairs = []
                    if k.layer == 3:
                        if n == 0:
                            wait(pe, ht_hi_ready, k.done(layers=L3, per=2))
                            wait(pe, ht_lo_ready, k.done(layers=L3, per=2))
                        pairs += [(ht_hi[:, f, c], ht_lo[:, f, c], w_hi[:, 3, f], w_lo[:, 3, f]) for f in range(FT)]
                    if n == 0:
                        wait(pe, t_hi_ready, k.done(per=2))
                        wait(pe, t_lo_ready, k.done(per=2))
                    w = {0: 0, 1: 1, 2: 2, 3: 4}[k.layer]
                    pairs += [(t_hi[:, k.odd, f, c], t_lo[:, k.odd, f, c], w_hi[:, w, f], w_lo[:, w, f]) for f in range(FT)]
                    product(O[:, k.odd, n], pairs).then_inc(o_ready, 1)

            for step in periods(pe):
                if step(1).valid:
                    gather(step(1))
                if step(2).layer == 0:
                    spread_scores(step(2))
                if step(0).valid:
                    project(step(0))

        def flat_blocks(t):
            flat = t.rearrange("p m n -> p (m n)")
            diag = t.rearrange("p m (b c) -> p (m b) c", b=NT)[:, 0:NT * NT:NT + 1]
            return diag, flat[:, P:NT * N - P]

        @block.scalar
        def _(act):
            for n in range(NW):
                b = (n + 1) % 2
                act.wait_ge(stage_in[b], 16 * ((n + 1) // 2 + 1))
                nc.scalar.copy(w_hi[:, n], stage[b]).then_inc(w_hi_ready, 1)

            def finish(k):
                if k.layer == 0:
                    for n in range(NT):
                        wait(act, o_ready, k.done(per=NT, part=n))
                        if n == 0:
                            free_act_out(act, k)
                        nc.scalar.activation(act_out[:, k.odd, n], O[:, k.odd, n], ACT.Exp).then_inc(exp_out_ready, 1)
                    for n in range(NT):
                        wait(act, exp_out_ready, k.done(layers=L0, per=NT, part=n))
                        nc.scalar.activation(act_out[:, k.odd, n], act_out[:, k.odd, n], ACT.Relu, bias=1.0,
                                             scale=-1.0).then_inc(elu_neg_ready, 1)
                if k.layer == 2:
                    for n in range(NT):
                        wait(act, o_ready, k.done(per=NT, part=n))
                        if n == 0:
                            free_act_out(act, k)
                            wait(act, row_mask_ready, k.done(layers=L2))
                        nc.scalar.activation(act_out[:, k.odd, n], O[:, k.odd, n], ACT.Relu,
                                             scale=row_mask[:, k.stream, n:n + 1]).then_inc(relu_ready, 1)

            def gather(k):
                wait(act, o_ready, k.done(2, per=NT))
                if k.layer == 3:
                    wait(act, recip_psum_ready, k.done(layers=L3))
                    wait(act, t_mean_ready, k.done(1, layers=L3, per=2))
                    nc.scalar.copy(recip_rows[:], recip_psum).then_inc(recip_rows_ready, 1)
                    for b in range(2):
                        wait(act, t_mean_ready, k.done(layers=L3, per=2, part=b))
                        c = slice(HALF * b, HALF * b + HALF)
                        nc.scalar.copy(t_hi[:, k.odd, c], t_mean[:, c]).then_inc(t_hi_ready, 1)
                    wait(act, o_ready, k.done_by_last(3, per=NT))
                    for half in range(2):
                        wait(act, ht_psum_ready, k.done(layers=L3, per=2, part=half))
                        nc.scalar.copy(ht_hi[:, HALF * half:HALF * half + HALF],
                                       X[:, 1 - half].rearrange("p (f n) -> p f n", f=HALF)).then_inc(ht_hi_ready, 1)
                    return
                for b in range(2):
                    wait(act, t_ready, k.done(per=2, part=b))
                    c = slice(HALF * b, HALF * b + HALF)
                    nc.scalar.copy(t_hi[:, k.odd, c], T[:, c]).then_inc(t_hi_ready, 1)

            def exps(k):
                wait(act, neg_ready, k.done(layers=L0))
                for m in range(NT):
                    nc.scalar.activation(scores[:, m], scores[:, m], ACT.Exp, bias=s_neg[:, m:m + 1],
                                         accum_out=s_sum[:, m:m + 1]).then_inc(exp_ready, 1)

            def prepare(k):
                if k.layer == 1:
                    diag, rest = flat_blocks(a_hi[:, k.stream])
                    raw_diag, raw_rest = flat_blocks(a_raw[:, k.stream])
                    wait(act, t_ready, k.done(8, per=2))
                    wait(act, a_loaded[k.stream], graph_turn(k, STREAMS))
                    nc.scalar.copy(rest, raw_rest).then_inc(ah_hi_ready, 1)
                    wait(act, diag_ready, k.done(layers=L1))
                    nc.scalar.copy(diag, a_diag[:]).then_inc(ah_hi_ready, 1)
                if k.layer == 2:
                    diag, _ = flat_blocks(a_hi[:, k.stream])
                    raw_diag, _ = flat_blocks(a_raw[:, k.stream])
                    wait(act, t_ready, k.done(4, per=2))
                    nc.scalar.copy(diag, raw_diag).then_inc(a_hi_ready, 1)
                wait(act, ln_ready, k.done())
                wait(act, h_lo_ready, k.done(2, per=NT))
                wait(act, wh_ready, k.done(2, layers=L0, per=DOTS))
                wait(act, ht_psum_ready, k.done(2, layers=L3, per=2))
                wait(act, t_ready, k.done(2, per=2))
                source = x_in[:, k.g0 % 2] if k.layer == 0 else xs[:, k.stream]
                for m in range(NT):
                    scale, shift = ln_scale[:, k.odd, m:m + 1], ln_bias[:, k.odd, m:m + 1]
                    total = h_sum[:, k.stream, m:m + 1] if k.layer == 2 else None
                    nc.scalar.activation(h[:, k.odd, m], source[:, m], ACT.Relu, bias=shift, scale=scale,
                                         accum_out=total).then_inc(h_ready, 1)
                    nc.scalar.activation(h_hi[:, k.odd, m], source[:, m], ACT.Relu, bias=shift,
                                         scale=scale).then_inc(h_hi_ready, 1)

            for step in periods(act):
                if step(-1).valid:
                    finish(step(-1))
                if step(1).valid:
                    gather(step(1))
                if step(2).layer == 0:
                    exps(step(2))
                if step(3).valid:
                    prepare(step(3))

        @block.vector
        def _(dve):
            for n in range(NW):
                b = (n + 1) % 2
                dve.wait_ge(w_hi_ready, n + 1)
                nc.vector.tensor_tensor(w_lo[:, n], stage[b], w_hi[:, n].bitcast(F32), ALU.subtract).then_inc(w_lo_ready, 1)
                if n == 0:
                    dve.wait_ge(v_psum_ready, 1)
                    nc.vector.tensor_copy(v_rows[:], X[:]).then_inc(v_ready, 1)

            def add_mask(k):
                wait(dve, wh_ready, k.done(layers=L0, per=DOTS))
                wait(dve, a_loaded[k.stream], graph_turn(k, STREAMS))
                nc.vector.tensor_scalar(mask_add[:], a_raw[:, k.stream], 0.5, MASKED, ALU.is_le,
                                        ALU.mult).then_inc(mask_ready, 1)

            def finish(k):
                if k.layer in (1, 3):
                    free_act_out(dve, k)
                for n in range(NT):
                    here, psum, state = act_out[:, k.odd, n], O[:, k.odd, n], xs[:, k.stream, n]
                    if k.layer != 2:
                        wait(dve, o_ready, k.done(per=NT, part=n))
                    if k.layer == 0:
                        wait(dve, exp_out_ready, k.done(layers=L0, per=NT, part=n))
                        nc.vector.scalar_tensor_tensor(state, psum, 0.0, x_in[:, k.g0 % 2, n], ALU.max,
                                                       ALU.add).then_inc(dve_finished, 1)
                    if k.layer == 1:
                        nc.vector.scalar_tensor_tensor(here, psum, deg_rsqrt[:, k.stream, n:n + 1], bias_rows[:],
                                                       ALU.mult, ALU.add).then_inc(affine_ready, 1)
                    if k.layer == 2:
                        wait(dve, relu_ready, k.done(layers=L2, per=NT, part=n))
                        nc.vector.tensor_tensor(state, here, state, ALU.add).then_inc(dve_finished, 1)
                    if k.layer == 3:
                        nc.vector.scalar_tensor_tensor(here, psum, 0.0, state, ALU.max, ALU.add).then_inc(dve_finished, 1)
                if k.layer == 1:
                    for n in range(NT):
                        wait(dve, affine_ready, k.done(layers=L1, per=NT, part=n))
                        nc.vector.scalar_tensor_tensor(xs[:, k.stream, n], act_out[:, k.odd, n], 0.0,
                                                       xs[:, k.stream, n], ALU.max, ALU.add).then_inc(dve_finished, 1)

            def mask_scores(k):
                wait(dve, mask_ready, k.done(layers=L0))
                wait(dve, wh_rows_ready, k.done(layers=L0))
                for m in range(NT):
                    nc.vector.scalar_tensor_tensor(scores[:, m], wh_rows, wh[:, k.g0 % 2, 1, m:m + 1], mask_add[:, m],
                                                   ALU.add, ALU.add).then_inc(scores_ready, 1)
                wait(dve, scores_ready, k.done(layers=L0, per=NT))
                nc.vector.scalar_tensor_tensor(scores[:], scores[:], SLOPE, scores[:], ALU.mult,
                                               ALU.max).then_inc(masked_ready, 1)
                wait(dve, masked_ready, k.done(layers=L0))
                nc.vector.tensor_reduce(s_neg[:], scores[:], AX.X, ALU.max, negate=True).then_inc(neg_ready, 1)

            def softmax_parts(k):
                wait(dve, exp_ready, k.done(layers=L0, per=NT))
                nc.vector.reciprocal(s_rec[:], s_sum[:]).then_inc(s_rec_ready, 1)
                wait(dve, s_rec_ready, k.done(layers=L0))
                wait(dve, t_ready, k.done_by_last(0, per=2))
                for m in range(NT):
                    nc.vector.tensor_scalar(p_hi[:, m], scores[:, m], s_rec[:, m:m + 1], None,
                                            ALU.mult).then_inc(p_hi_ready, 1)
                for m in range(NT):
                    wait(dve, p_hi_ready, k.done(layers=L0, per=NT, part=m))
                    nc.vector.scalar_tensor_tensor(p_lo[:, m], scores[:, m], s_rec[:, m:m + 1],
                                                   p_hi[:, m].bitcast(F32), ALU.mult, ALU.subtract).then_inc(p_lo_ready, 1)

            def gather(k):
                if k.layer == 3:
                    wait(dve, recip_rows_ready, k.done(layers=L3))
                    wait(dve, t_hi_ready, k.done(1, per=2))
                    for b in range(2):
                        c = slice(HALF * b, HALF * b + HALF)
                        wait(dve, t_ready, k.done(per=2, part=b))
                        nc.vector.tensor_tensor(t_mean[:, c], T[:, c], recip_rows[:].unsqueeze(1).to_broadcast([P, HALF, N]),
                                                ALU.mult).then_inc(t_mean_ready, 1)
                for b in range(2):
                    c = slice(HALF * b, HALF * b + HALF)
                    whole = t_mean if k.layer == 3 else T
                    wait(dve, t_hi_ready, k.done(per=2, part=b))
                    nc.vector.tensor_tensor(t_lo[:, k.odd, c], whole[:, c], t_hi[:, k.odd, c].bitcast(F32),
                                            ALU.subtract).then_inc(t_lo_ready, 1)
                if k.layer == 3:
                    for half in range(2):
                        transposed(k, half)

            def transposed(k, half):
                c = slice(HALF * half, HALF * half + HALF)
                wait(dve, ht_hi_ready, k.done(layers=L3, per=2, part=half))
                nc.vector.tensor_tensor(ht_lo[:, c], X[:, 1 - half].rearrange("p (f n) -> p f n", f=HALF),
                                        ht_hi[:, c].bitcast(F32), ALU.subtract).then_inc(ht_lo_ready, 1)

            def degrees(k):
                wait(dve, rows_loaded, k.affine(lambda i: 16 * (plan.graph(i) + 1)))
                nc.vector.tensor_reduce(deg[:, k.stream], a_rows[:], AX.X, ALU.add).then_inc(deg_ready, 1)
                wait(dve, deg_ready, k.done(layers=L0))
                nc.vector.tensor_scalar(deg_floor[:, k.stream], deg[:, k.stream], DEG_EPS, None,
                                        ALU.max).then_inc(deg_floor_ready, 1)
                wait(dve, deg_floor_ready, k.done(layers=L0))
                nc.vector.reciprocal(deg_recip[:, k.stream], deg_floor[:, k.stream]).then_inc(deg_recip_ready, 1)

            def statistics(k):
                if k.layer == 0:
                    source = x_in[:, k.g0 % 2]
                    wait(dve, x_loaded[k.g0 % 2], graph_turn(k, 2))
                else:
                    source = xs[:, k.stream]
                    if k.layer == 1:
                        wait(dve, elu_ready, k.done(4, layers=L0, per=NT))
                    else:
                        wait(dve, dve_finished, k.done(4, per=NT))
                wait(dve, ln_ready, k.done(2))
                for m in range(NT):
                    nc.vector.bn_stats(ln_stats[:, k.odd, m], source[:, m]).then_inc(stats_ready, 1)
                wait(dve, stats_ready, k.done(per=NT))
                nc.vector.memset(carrier[:], 0.0)
                for m in range(NT):
                    nc.vector.bn_aggr(ln_mv[:, k.odd, m], ln_stats[:, k.odd, m]).then_inc(mv_ready, 1)

            def prepare(k):
                if k.layer == 1:
                    diag, rest = flat_blocks(a_lo[:, k.stream])
                    hi_diag, hi_rest = flat_blocks(a_hi[:, k.stream].bitcast(F32))
                    raw_diag, raw_rest = flat_blocks(a_raw[:, k.stream])
                    wait(dve, ah_hi_ready, k.done(1, layers=L1, per=2))
                    nc.vector.tensor_tensor(a_diag[:], raw_diag, ident[:].unsqueeze(1).to_broadcast([P, NT, P]),
                                            ALU.add).then_inc(diag_ready, 1)
                    wait(dve, ah_hi_ready, k.done(layers=L1, per=2, part=0))
                    nc.vector.tensor_tensor(rest, raw_rest, hi_rest, ALU.subtract).then_inc(ah_lo_ready, 1)
                    wait(dve, ah_hi_ready, k.done(layers=L1, per=2, part=1))
                    nc.vector.tensor_tensor(diag, a_diag[:], hi_diag, ALU.subtract).then_inc(ah_lo_ready, 1)
                if k.layer == 2:
                    diag, _ = flat_blocks(a_lo[:, k.stream])
                    hi_diag, _ = flat_blocks(a_hi[:, k.stream].bitcast(F32))
                    raw_diag, _ = flat_blocks(a_raw[:, k.stream])
                    wait(dve, a_hi_ready, k.done(layers=L2))
                    nc.vector.tensor_tensor(diag, raw_diag, hi_diag, ALU.subtract).then_inc(a_lo_ready, 1)
                    wait(dve, h_ready, k.done(per=NT))
                    nc.vector.tensor_scalar(row_mask[:, k.stream], h_sum[:, k.stream], 0.0, None,
                                            ALU.is_gt).then_inc(row_mask_ready, 1)
                if k.layer == 0:
                    for m in range(NT):
                        wait(dve, h_ready, k.done(per=NT, part=m))
                        for v in range(2):
                            n = 2 * m + v
                            wait(dve, wh_ready, k.done(layers=L0, per=DOTS, part=n - 2) if n >= 2
                                 else k.done(1, layers=L0, per=DOTS))
                            nc.vector.tensor_tensor_reduce(
                                out=(scores, mask_add)[v][:].rearrange("p m n -> p (m n)"), in0=h[:, k.odd, m],
                                in1=v_rows[:, v], scale=1.0, scalar=0.0, op0=ALU.mult, op1=ALU.add,
                                accum_out=wh[:, k.g0 % 2, v, m:m + 1]).then_inc(wh_ready, 1)

            for step in periods(dve):
                if step(2).layer == 0:
                    add_mask(step(2))
                if step(-1).valid:
                    finish(step(-1))
                if step(2).layer == 0:
                    mask_scores(step(2))
                if step(1).valid:
                    gather(step(1))
                if step(2).layer == 0:
                    softmax_parts(step(2))
                    degrees(step(2))
                if step(3).valid:
                    statistics(step(3))
                    prepare(step(3))

        @block.gpsimd
        def _(pool):
            nc.gpsimd.memset(ident[:], 0.0).then_inc(ident_zero, 1)
            for tile, value in ((minus_half, -0.5), (ones, 1.0), (ln_eps, LN_EPS), (minus_one, -1.0)):
                nc.gpsimd.memset(tile[:], value).then_inc(columns_ready, 1)
            pool.wait_ge(ident_zero, 1)
            nc.gpsimd.affine_select(out=ident[:], in_=ident[:], compare_op=ALU.not_equal, fill=1.0, base=0,
                                    pattern=[[-1, P]], channel_multiplier=1).then_inc(ident_ready, 1)
            pool.wait_ge(columns_ready, 4)

            def finish(k):
                if k.layer == 0:
                    for n in range(NT):
                        wait(pool, dve_finished, k.done(per=NT, part=n))
                        wait(pool, elu_neg_ready, k.done(layers=L0, per=NT, part=n))
                        nc.gpsimd.tensor_tensor(xs[:, k.stream, n], xs[:, k.stream, n], act_out[:, k.odd, n],
                                                ALU.subtract).then_inc(elu_ready, 1)

            def degrees(k):
                wait(pool, deg_ready, k.done(layers=L0))
                nc.gpsimd.tensor_tensor(deg_one[:, k.stream], deg[:, k.stream], ones[:], ALU.add).then_inc(deg_one_ready, 1)
                wait(pool, deg_one_ready, k.done(layers=L0))
                nc.gpsimd.tensor_tensor(deg_rsqrt[:, k.stream], deg_one[:, k.stream], minus_half[:],
                                        ALU.pow).then_inc(deg_rsqrt_ready, 1)

            def prepare(k):
                b = k.odd
                wait(pool, h_ready, k.done(2, per=NT))
                wait(pool, h_hi_ready, k.done(2, per=NT))
                wait(pool, mv_ready, k.done(per=NT))
                nc.gpsimd.tensor_tensor(ln_var[:, b], ln_mv[:, b, :, 1], ln_eps[:], ALU.add).then_inc(ln_part, 1)
                wait(pool, ln_part, k.done(per=3, part=0))
                scale = ln_rstd[:, b] if k.layer == 1 else ln_scale[:, b]
                nc.gpsimd.tensor_tensor(scale, ln_var[:, b], minus_half[:], ALU.pow).then_inc(ln_part, 1)
                wait(pool, ln_part, k.done(per=3, part=1))
                if k.layer == 1:
                    wait(pool, deg_rsqrt_ready, k.done(layers=L0))
                    nc.gpsimd.tensor_tensor(ln_scale[:, b], ln_rstd[:, b], deg_rsqrt[:, k.stream],
                                            ALU.mult).then_inc(ln_scaled, 1)
                    wait(pool, ln_scaled, k.done(layers=L1))
                nc.gpsimd.tensor_tensor(ln_ms[:, b], ln_mv[:, b, :, 0], ln_scale[:, b], ALU.mult).then_inc(ln_part, 1)
                wait(pool, ln_part, k.done(per=3, part=2))
                nc.gpsimd.tensor_tensor(ln_bias[:, b], ln_ms[:, b], minus_one[:], ALU.mult).then_inc(ln_ready, 1)
                for m in range(NT):
                    wait(pool, h_ready, k.done(per=NT, part=m))
                    wait(pool, h_hi_ready, k.done(per=NT, part=m))
                    wait(pool, t_ready, k.done(2, per=2))
                    nc.gpsimd.tensor_tensor(h_lo[:, b, m], h[:, b, m], h_hi[:, b, m].bitcast(F32),
                                            ALU.subtract).then_inc(h_lo_ready, 1)

            for step in periods(pool):
                if step(-1).valid:
                    finish(step(-1))
                if step(2).layer == 0:
                    degrees(step(2))
                if step(3).valid:
                    prepare(step(3))


def kernel(x, adj, L0_gnn_W, L0_gnn_a, L1_gnn_kernel, L1_gnn_bias, L2_gnn_kernel, L3_gnn_W):
    import numpy as np
    import concourse.bacc as bacc
    from concourse.bass_utils import run_bass_kernel_spmd

    x, adj = np.asarray(x), np.asarray(adj)
    w3_t = np.asarray(L3_gnn_W).T
    f = x.shape[-1]
    arrays = {
        "x": np.ascontiguousarray(x),
        "adj": np.ascontiguousarray(adj),
        "adj_t": np.ascontiguousarray(adj.transpose(0, 2, 1)),
        "w_all": np.ascontiguousarray(np.stack([np.asarray(L0_gnn_W), np.asarray(L1_gnn_kernel),
                                                np.asarray(L2_gnn_kernel), w3_t[:f], w3_t[f:]])),
        "w0_t": np.ascontiguousarray(np.asarray(L0_gnn_W).T),
        "a_cols": np.ascontiguousarray(np.asarray(L0_gnn_a).reshape(2, f // 128, 128).transpose(2, 0, 1)),
        "bias": np.ascontiguousarray(np.asarray(L1_gnn_bias)),
    }
    nc = bacc.Bacc("TRN2", target_bir_lowering=False, num_devices=1)
    aps = {n: nc.dram_tensor(n, a.shape, F32, kind="ExternalInput").ap() for n, a in arrays.items()}
    out = nc.dram_tensor("out", x.shape, F32, kind="ExternalOutput").ap()
    gnn_kernel(nc, out=out, **aps)
    r = run_bass_kernel_spmd(nc, [arrays], core_ids=[0])
    return r.results[0]["out"]
```

```python
from contextlib import ExitStack

import concourse.bass as bass
from concourse import mybir

F32 = mybir.dt.float32
F32R = mybir.dt.float32r
ALU = mybir.AluOpType
ACT = mybir.ActivationFunctionType
AX = mybir.AxisListType

P = 128
LAYERS = 4
STREAMS = 4
MASKED = -9000000000000000.0
SLOPE = 0.2
LN_EPS = 1e-5
DEG_EPS = 1e-6
WEIGHTS = 5


class Schedule:

    def __init__(self, graphs):
        self.graphs = graphs
        self.turns = graphs // STREAMS
        self.rounds = LAYERS * self.turns + STREAMS - 1
        self.steps = STREAMS * self.rounds
        self.span = STREAMS * LAYERS
        self.first, self.last = -3, self.steps
        self.loop_at = self.span + STREAMS + 1
        whole = next(k for k in range(self.span, self.steps) if not self.valid(k))
        self.loops = (whole - 3 - self.loop_at) // self.span

    @staticmethod
    def late(stream):
        return -stream % STREAMS

    def valid(self, k):
        s, r = k % STREAMS, k // STREAMS
        return 0 <= k < self.steps and 0 <= r - self.late(s) < LAYERS * self.turns

    def layer(self, k):
        return (k // STREAMS + k % STREAMS) % LAYERS if self.valid(k) else None

    def graph(self, k):
        s, r = k % STREAMS, k // STREAMS
        return STREAMS * ((r - self.late(s)) // LAYERS) + self.late(s)

    def count(self, k, layers=range(LAYERS)):
        return sum(self.layer(i) in layers for i in range(k + 1) if self.valid(i))


class Step:

    def __init__(self, plan, k, turn):
        self.plan, self.k, self.turn = plan, k, turn
        self.valid, self.layer = plan.valid(k), plan.layer(k)
        self.stream = k % STREAMS
        self.odd = k % 2
        self.g0 = plan.graph(k) if self.valid else None

    def affine(self, value_at):
        base = value_at(self.k)
        if self.turn is None:
            return base
        slope = value_at(self.k + self.plan.span) - base
        for i in range(self.plan.loops):
            assert value_at(self.k + i * self.plan.span) == base + slope * i
        assert base > 0 or slope == 0, "a wait below one in the loop's first turn"
        return base + slope * self.turn if slope else base

    def graph(self, ahead=0):
        g = self.g0 + ahead
        return g if self.turn is None else g + STREAMS * self.turn

    def done(self, back=0, layers=range(LAYERS), per=1, part=None):
        def value_at(k):
            k -= back
            if part is None:
                return per * self.plan.count(k, layers)
            return per * self.plan.count(k - 1, layers) + (part + 1 if self.plan.layer(k) in layers else 0)
        return self.affine(value_at)

    def done_by_last(self, layer, per=1):
        def value_at(k):
            before = [i for i in range(k) if self.plan.layer(i) == layer]
            return per * self.plan.count(before[-1]) if before else 0
        return self.affine(value_at)


class Period:

    def __init__(self, plan, j, turn):
        self.plan, self.j, self.turn = plan, j, turn
        self.half = j + 3 if 0 <= j + 3 < 2 * WEIGHTS else None

    def __call__(self, n):
        return Step(self.plan, self.j + n, self.turn)


def gnn_kernel(nc, x, adj, adj_t, w_all, a_vecs, bias, out):
    G, N, F = x.shape
    NT = N // P
    FT = F // P
    HALF = FT // NT
    plan = Schedule(G)
    L0, L1, L2, L3, L012 = (0,), (1,), (2,), (3,), (0, 1, 2)
    DOTS = 2 * NT

    with ExitStack() as ctx:
        def sb(name, shape, dt=F32):
            return ctx.enter_context(nc.sbuf_tensor(name, shape, dt))

        def sem(name):
            return ctx.enter_context(nc.semaphore(name))

        w_hi = sb("w_hi", [P, WEIGHTS, FT, F], F32R)
        w_lo = sb("w_lo", [P, WEIGHTS, FT, F], F32R)
        v_rows = sb("v_rows", [P, 2, F])
        bias_rows = sb("bias_rows", [P, F])
        ident = sb("ident", [P, P])
        minus_half, ones, ln_eps, minus_one = (sb(n, [P, NT]) for n in ("minus_half", "ones", "ln_eps", "minus_one"))
        carrier = sb("carrier", [P, 1])
        v_cols = sb("v_cols", [P, 2, FT])
        xs = sb("xs", [P, STREAMS, NT, F])
        a_raw = sb("a_raw", [P, STREAMS, NT, N])
        a_hi = sb("a_hi", [P, STREAMS, NT, N], F32R)
        a_lo = sb("a_lo", [P, STREAMS, NT, N], F32R)
        deg = sb("deg", [P, STREAMS, NT])
        deg_one = sb("deg_one", [P, STREAMS, NT])
        deg_rsqrt = sb("deg_rsqrt", [P, STREAMS, NT])
        deg_floor = sb("deg_floor", [P, STREAMS, NT])
        deg_recip = sb("deg_recip", [P, STREAMS, NT])
        x_in = sb("x_in", [P, 2, NT, F])
        a_rows = sb("a_rows", [P, NT, N])
        a_diag = sb("a_diag", [P, NT, P])
        h = sb("h", [P, 2, NT, F])
        h_hi = sb("h_hi", [P, 2, NT, F], F32R)
        h_lo = sb("h_lo", [P, 2, NT, F], F32R)
        t_hi = sb("t_hi", [P, 2, FT, N], F32R)
        t_lo = sb("t_lo", [P, 2, FT, N], F32R)
        t_mean = sb("t_mean", [P, FT, N])
        ht_hi = sb("ht_hi", [P, FT, N], F32R)
        ht_lo = sb("ht_lo", [P, FT, N], F32R)
        recip_rows = sb("recip_rows", [P, N])
        act_out = sb("act_out", [P, 2, NT, F])
        scores = sb("scores", [P, NT, N])
        mask_add = sb("mask_add", [P, NT, N])
        p_hi = sb("p_hi", [P, NT, N], F32R)
        p_lo = sb("p_lo", [P, NT, N], F32R)
        ln_stats = sb("ln_stats", [P, 2, NT, 6])
        ln_mv = sb("ln_mv", [P, 2, NT, 2])
        ln_var = sb("ln_var", [P, 2, NT])
        ln_rstd = sb("ln_rstd", [P, 2, NT])
        ln_scale = sb("ln_scale", [P, 2, NT])
        ln_ms = sb("ln_ms", [P, 2, NT])
        ln_bias = sb("ln_bias", [P, 2, NT])
        h_sum = sb("h_sum", [P, STREAMS, NT])
        row_mask = sb("row_mask", [P, STREAMS, NT])
        wh = sb("wh", [P, 2, 2, NT])
        s_neg = sb("s_neg", [P, NT])
        s_sum = sb("s_sum", [P, NT])
        s_rec = sb("s_rec", [P, NT])

        T = ctx.enter_context(nc.psum_tensor("T", [P, FT, N], F32))
        O = ctx.enter_context(nc.psum_tensor("O", [P, 2, NT, F], F32))
        X = ctx.enter_context(nc.psum_tensor("X", [P, 2, F], F32))
        wh_rows = X[:, 0, 0:N]
        recip_psum = X[:, 0, 0:N]

        stage = [xs[:, 1], xs[:, 2], t_mean[:].rearrange("p (c f) n -> p c (f n)", c=HALF)]

        def half_weight(i):
            return i // 2, slice(HALF * (i % 2), HALF * (i % 2) + HALF)

        stage_in = [sem(f"stage_in{b}") for b in range(len(stage))]
        vectors_in, bias_in = sem("vectors_in"), sem("bias_in")
        x_loaded = [sem(f"x_loaded{b}") for b in range(2)]
        a_loaded = [sem(f"a_loaded{s}") for s in range(STREAMS)]
        rows_loaded = sem("rows_loaded")
        out_stored = [sem(f"out_stored{b}") for b in range(2)]
        w_hi_ready, w_lo_ready = sem("w_hi_ready"), sem("w_lo_ready")
        v_cols_ready, v_psum_ready, v_ready = sem("v_cols_ready"), sem("v_psum_ready"), sem("v_ready")
        ident_zero, ident_ready, columns_ready = sem("ident_zero"), sem("ident_ready"), sem("columns_ready")
        t_ready, o_ready = sem("t_ready"), sem("o_ready")
        wh_rows_ready, recip_psum_ready, ht_psum_ready = sem("wh_rows_ready"), sem("recip_psum_ready"), sem("ht_psum_ready")
        stats_ready, mv_ready, ln_part, ln_scaled, ln_ready = (
            sem("stats_ready"), sem("mv_ready"), sem("ln_part"), sem("ln_scaled"), sem("ln_ready"))
        h_ready, h_hi_ready, h_lo_ready, row_mask_ready = (
            sem("h_ready"), sem("h_hi_ready"), sem("h_lo_ready"), sem("row_mask_ready"))
        deg_ready, deg_one_ready, deg_rsqrt_ready, deg_floor_ready, deg_recip_ready = (
            sem("deg_ready"), sem("deg_one_ready"), sem("deg_rsqrt_ready"), sem("deg_floor_ready"), sem("deg_recip_ready"))
        diag_ready, ah_hi_ready, ah_lo_ready, a_hi_ready, a_lo_ready = (
            sem("diag_ready"), sem("ah_hi_ready"), sem("ah_lo_ready"), sem("a_hi_ready"), sem("a_lo_ready"))
        wh_ready, mask_ready, scores_ready, masked_ready, neg_ready, exp_ready, s_rec_ready, p_hi_ready, p_lo_ready = (
            sem("wh_ready"), sem("mask_ready"), sem("scores_ready"), sem("masked_ready"), sem("neg_ready"),
            sem("exp_ready"), sem("s_rec_ready"), sem("p_hi_ready"), sem("p_lo_ready"))
        t_hi_ready, t_lo_ready, mean_lo_ready, t_mean_ready, recip_rows_ready, ht_hi_ready, ht_lo_ready = (
            sem("t_hi_ready"), sem("t_lo_ready"), sem("mean_lo_ready"), sem("t_mean_ready"), sem("recip_rows_ready"),
            sem("ht_hi_ready"), sem("ht_lo_ready"))
        exp_out_ready, elu_neg_ready, affine_ready, relu_ready, dve_finished, elu_ready = (
            sem("exp_out_ready"), sem("elu_neg_ready"), sem("affine_ready"), sem("relu_ready"),
            sem("dve_finished"), sem("elu_ready"))

        def periods(eng):
            for j in range(plan.first, plan.loop_at):
                yield Period(plan, j, None)
            with eng.Fori(0, plan.loops) as turn:
                for j in range(plan.loop_at, plan.loop_at + plan.span):
                    yield Period(plan, j, turn)
            for j in range(plan.loop_at + plan.span * plan.loops, plan.last + 2):
                yield Period(plan, j, None)

        def wait(eng, semaphore, value):
            if isinstance(value, int) and value <= 0:
                return
            eng.wait_ge(semaphore, value)

        def tiles(dram, g):
            return dram[g].rearrange("(m p) f -> p m f", p=P)

        def graph_turn(step, every, ahead=0):
            return step.affine(lambda k: 16 * ((plan.graph(k) + ahead) // every + 1))

        def free_act_out(eng, k):
            wait(eng, elu_ready, k.done(2, layers=L0, per=NT))
            wait(eng, dve_finished, k.done(2, per=NT))
            wait(eng, out_stored[k.odd], k.affine(lambda i: 16 * sum(
                plan.layer(e) == 3 for e in range(i - 1) if e % 2 == i % 2)))

        block = ctx.enter_context(nc.Block())

        @block.sync
        def _(sp):
            def load_half(i):
                w, c = half_weight(i)
                b = i % len(stage)
                if i >= len(stage):
                    sp.wait_ge(w_lo_ready, i - len(stage) + 1)
                sp.dma_start(stage[b], w_all[w].rearrange("(c p) n -> p c n", p=P)[:, c]).then_inc(stage_in[b], 16)

            sp.dma_start(v_rows[:].rearrange("p v n -> p (v n)"),
                         a_vecs.rearrange("v n -> (v n)").partition_broadcast(P)).then_inc(vectors_in, 16)
            load_half(0)
            load_half(1)
            for g in range(2):
                s = -g % STREAMS
                sp.dma_start(x_in[:, g], tiles(x, g)).then_inc(x_loaded[g], 16)
                sp.dma_start(a_raw[:, s], tiles(adj_t, g)).then_inc(a_loaded[s], 16)
            sp.dma_start(a_rows[:], tiles(adj, 0)).then_inc(rows_loaded, 16)
            sp.dma_start(bias_rows[:], bias.partition_broadcast(P)).then_inc(bias_in, 16)
            load_half(2)
            for g in range(2, STREAMS):
                s = -g % STREAMS
                sp.dma_start(a_raw[:, s], tiles(adj_t, g)).then_inc(a_loaded[s], 16)

            for step in periods(sp):
                if step.half is not None and step.half > 2:
                    load_half(step.half)
                done = step(-1)
                if done.layer == 3:
                    sp.wait_ge(dve_finished, done.done(per=NT))
                    sp.dma_start(tiles(out, done.graph()), act_out[:, done.odd]).then_inc(out_stored[done.stream % 2], 16)
                if done.layer == 0 and done.g0 + 2 < G:
                    sp.wait_ge(dve_finished, done.done(per=NT))
                    sp.dma_start(x_in[:, done.stream % 2], tiles(x, done.graph(2))).then_inc(x_loaded[done.stream % 2], 16)
                att = step(2)
                if att.layer == 0 and att.g0 + 1 < G:
                    sp.wait_ge(deg_ready, att.done(layers=L0))
                    sp.dma_start(a_rows[:], tiles(adj, att.graph(1))).then_inc(rows_loaded, 16)
                pre = step(3)
                if pre.layer == 2 and pre.g0 + STREAMS < G:
                    sp.wait_ge(a_lo_ready, pre.done(layers=L2))
                    sp.dma_start(a_raw[:, pre.stream], tiles(adj_t, pre.graph(STREAMS))).then_inc(a_loaded[pre.stream], 16)
            for b in range(2):
                sp.wait_ge(out_stored[b], 16 * (G // 2))

        @block.tensor
        def _(pe):
            def product(psum, pairs):
                last = None
                for n, (s_hi, s_lo, m_hi, m_lo) in enumerate(pairs):
                    for i, (s, m) in enumerate(((s_hi, m_hi), (s_hi, m_lo), (s_lo, m_hi))):
                        last = nc.tensor.matmul(psum, s, m, start=(n == 0 and i == 0),
                                                stop=(n == len(pairs) - 1 and i == 2))
                return last

            pe.wait_ge(ident_ready, 1)
            pe.wait_ge(v_cols_ready, 2 * FT)
            for v in range(2):
                for c in range(FT):
                    last = nc.tensor.transpose(X[:, v, c * P:c * P + P], v_cols[:, v, c:c + 1].to_broadcast([P, P]), ident[:])
            last.then_inc(v_psum_ready, 1)
            pe.wait_ge(v_ready, 1)

            def transpose_h(k, half):
                if half == 1:
                    wait(pe, recip_rows_ready, k.done(layers=L3))
                    wait(pe, scores_ready, k.done(-1, layers=L0, per=NT))
                for f in range(HALF * half, HALF * half + HALF):
                    for m in range(NT):
                        c = (f % HALF) * N + m * P
                        last = nc.tensor.transpose(X[:, 1 - half, c:c + P], h[:, k.odd, m, f * P:f * P + P], ident[:])
                last.then_inc(ht_psum_ready, 1)

            def gather(k):
                if k.layer == 3:
                    wait(pe, deg_recip_ready, k.done(layers=L0))
                    wait(pe, scores_ready, k.done(layers=L0, per=NT))
                    wait(pe, ht_lo_ready, k.done(1, layers=L3, per=2))
                    for m in range(NT):
                        last = nc.tensor.transpose(recip_psum[:, m * P:m * P + P],
                                                   deg_recip[:, k.stream, m:m + 1].to_broadcast([P, P]), ident[:])
                    last.then_inc(recip_psum_ready, 1)
                    wait(pe, h_ready, k.done(per=NT))
                    transpose_h(k, 0)
                wait(pe, h_hi_ready, k.done(per=NT))
                wait(pe, h_lo_ready, k.done(per=NT))
                if k.layer == 0:
                    wait(pe, p_lo_ready, k.done(layers=L0, per=NT))
                    m_hi, m_lo = p_hi, p_lo
                else:
                    m_hi, m_lo = a_hi[:, k.stream], a_lo[:, k.stream]
                if k.layer == 1:
                    wait(pe, ah_hi_ready, k.done(layers=L1, per=2))
                    wait(pe, ah_lo_ready, k.done(layers=L1, per=2))
                if k.layer == 2:
                    wait(pe, a_hi_ready, k.done(layers=L2))
                    wait(pe, a_lo_ready, k.done(layers=L2))
                for b in range(2):
                    wait(pe, t_lo_ready, k.done(1, layers=L012, per=2, part=b))
                    wait(pe, t_mean_ready, k.done(1, layers=L3, per=2, part=b))
                    for f in range(HALF * b, HALF * b + HALF):
                        c = slice(f * P, f * P + P)
                        last = product(T[:, f], [(h_hi[:, k.odd, m, c], h_lo[:, k.odd, m, c], m_hi[:, m], m_lo[:, m])
                                                 for m in range(NT)])
                    last.then_inc(t_ready, 1)

            def spread_scores(k):
                wait(pe, wh_ready, k.done(layers=L0, per=DOTS))
                wait(pe, scores_ready, k.done(1, layers=L0, per=NT))
                wait(pe, ht_lo_ready, k.done(2, layers=L3, per=2))
                wait(pe, recip_rows_ready, k.done(1, layers=L3))
                for m in range(NT):
                    last = nc.tensor.transpose(wh_rows[:, m * P:m * P + P],
                                               wh[:, k.g0 % 2, 0, m:m + 1].to_broadcast([P, P]), ident[:])
                last.then_inc(wh_rows_ready, 1)

            def project(k, following):
                w = {0: 0, 1: 1, 2: 2, 3: 4}[k.layer]
                if k.turn is None:
                    wait(pe, w_lo_ready, 2 * w + 2)
                for n in range(NT):
                    if n == 1 and following.layer == 3:
                        transpose_h(following, 1)
                    c = slice(n * P, n * P + P)
                    wait(pe, dve_finished, k.done(2, per=NT, part=n))
                    pairs = []
                    if k.layer == 3:
                        if n == 0:
                            wait(pe, ht_hi_ready, k.done(layers=L3, per=2))
                            wait(pe, ht_lo_ready, k.done(layers=L3, per=2))
                        pairs += [(ht_hi[:, f, c], ht_lo[:, f, c], w_hi[:, 3, f], w_lo[:, 3, f]) for f in range(FT)]
                    if n == 0:
                        wait(pe, t_hi_ready, k.done(per=2))
                        wait(pe, *((mean_lo_ready, k.done(layers=L3, per=2)) if k.layer == 3 else
                                   (t_lo_ready, k.done(layers=L012, per=2))))
                    pairs += [(t_hi[:, k.odd, f, c], t_lo[:, k.odd, f, c], w_hi[:, w, f], w_lo[:, w, f]) for f in range(FT)]
                    product(O[:, k.odd, n], pairs).then_inc(o_ready, 1)

            for step in periods(pe):
                if step(1).valid:
                    gather(step(1))
                if step(2).layer == 0:
                    spread_scores(step(2))
                if step(0).valid:
                    project(step(0), step(1))
                elif step(1).layer == 3:
                    transpose_h(step(1), 1)

        def flat_blocks(t):
            flat = t.rearrange("p m n -> p (m n)")
            diag = t.rearrange("p m (b c) -> p (m b) c", b=NT)[:, 0:NT * NT:NT + 1]
            return diag, flat[:, P:NT * N - P]

        @block.scalar
        def _(act):
            def split_weight(i):
                w, c = half_weight(i)
                b = i % len(stage)
                act.wait_ge(stage_in[b], 16 * (i // len(stage) + 1))
                nc.scalar.copy(w_hi[:, w, c], stage[b]).then_inc(w_hi_ready, 1)

            def spread_recip(k):
                wait(act, recip_psum_ready, k.done(layers=L3))
                wait(act, mean_lo_ready, k.done(1, layers=L3, per=2))
                nc.scalar.copy(recip_rows[:], recip_psum).then_inc(recip_rows_ready, 1)

            def finish(k):
                if k.layer == 0:
                    for n in range(NT):
                        wait(act, o_ready, k.done(per=NT, part=n))
                        if n == 0:
                            free_act_out(act, k)
                        nc.scalar.activation(act_out[:, k.odd, n], O[:, k.odd, n], ACT.Exp).then_inc(exp_out_ready, 1)
                    for n in range(NT):
                        wait(act, exp_out_ready, k.done(layers=L0, per=NT, part=n))
                        nc.scalar.activation(act_out[:, k.odd, n], act_out[:, k.odd, n], ACT.Relu, bias=1.0,
                                             scale=-1.0).then_inc(elu_neg_ready, 1)
                if k.layer == 2:
                    for n in range(NT):
                        wait(act, o_ready, k.done(per=NT, part=n))
                        if n == 0:
                            free_act_out(act, k)
                            wait(act, row_mask_ready, k.done(layers=L2))
                        nc.scalar.activation(act_out[:, k.odd, n], O[:, k.odd, n], ACT.Relu,
                                             scale=row_mask[:, k.stream, n:n + 1]).then_inc(relu_ready, 1)

            def gather(k):
                wait(act, o_ready, k.done(2, per=NT))
                if k.layer == 3:
                    wait(act, o_ready, k.done_by_last(3, per=NT))
                    transposed(k, 0)
                    for b in range(2):
                        wait(act, t_mean_ready, k.done(layers=L3, per=2, part=b))
                        c = slice(HALF * b, HALF * b + HALF)
                        nc.scalar.copy(t_hi[:, k.odd, c], t_mean[:, c]).then_inc(t_hi_ready, 1)
                    return
                for b in range(2):
                    wait(act, t_ready, k.done(per=2, part=b))
                    c = slice(HALF * b, HALF * b + HALF)
                    nc.scalar.copy(t_hi[:, k.odd, c], T[:, c]).then_inc(t_hi_ready, 1)

            def transposed(k, half):
                wait(act, ht_psum_ready, k.done(layers=L3, per=2, part=half))
                nc.scalar.copy(ht_hi[:, HALF * half:HALF * half + HALF],
                               X[:, 1 - half].rearrange("p (f n) -> p f n", f=HALF)).then_inc(ht_hi_ready, 1)

            def exps(k):
                wait(act, neg_ready, k.done(layers=L0))
                for m in range(NT):
                    nc.scalar.activation(scores[:, m], scores[:, m], ACT.Exp, bias=s_neg[:, m:m + 1],
                                         accum_out=s_sum[:, m:m + 1]).then_inc(exp_ready, 1)

            def prepare(k):
                if k.layer == 1:
                    diag, rest = flat_blocks(a_hi[:, k.stream])
                    raw_diag, raw_rest = flat_blocks(a_raw[:, k.stream])
                    wait(act, t_ready, k.done(8, per=2))
                    wait(act, a_loaded[k.stream], graph_turn(k, STREAMS))
                    nc.scalar.copy(rest, raw_rest).then_inc(ah_hi_ready, 1)
                    wait(act, diag_ready, k.done(layers=L1))
                    nc.scalar.copy(diag, a_diag[:]).then_inc(ah_hi_ready, 1)
                if k.layer == 2:
                    diag, _ = flat_blocks(a_hi[:, k.stream])
                    raw_diag, _ = flat_blocks(a_raw[:, k.stream])
                    wait(act, t_ready, k.done(4, per=2))
                    nc.scalar.copy(diag, raw_diag).then_inc(a_hi_ready, 1)

            def activate(k):
                wait(act, ln_ready, k.done())
                wait(act, h_lo_ready, k.done(2, per=NT))
                wait(act, wh_ready, k.done(2, layers=L0, per=DOTS))
                wait(act, ht_psum_ready, k.done(2, layers=L3, per=2))
                wait(act, t_ready, k.done(2, per=2))
                source = x_in[:, k.g0 % 2] if k.layer == 0 else xs[:, k.stream]
                for m in range(NT):
                    scale, shift = ln_scale[:, k.odd, m:m + 1], ln_bias[:, k.odd, m:m + 1]
                    total = h_sum[:, k.stream, m:m + 1] if k.layer == 2 else None
                    nc.scalar.activation(h[:, k.odd, m], source[:, m], ACT.Relu, bias=shift, scale=scale,
                                         accum_out=total).then_inc(h_ready, 1)
                    nc.scalar.activation(h_hi[:, k.odd, m], source[:, m], ACT.Relu, bias=shift,
                                         scale=scale).then_inc(h_hi_ready, 1)

            for step in periods(act):
                if step(1).layer == 3:
                    spread_recip(step(1))
                if step(2).layer in (1, 2, 3):
                    activate(step(2))
                if step(-1).valid:
                    finish(step(-1))
                if step(1).valid:
                    gather(step(1))
                if step(2).layer == 0:
                    exps(step(2))
                if step(1).layer == 3:
                    transposed(step(1), 1)
                if step(3).layer == 0:
                    activate(step(3))
                if step(3).valid:
                    prepare(step(3))
                if step.half is not None:
                    split_weight(step.half)

        @block.vector
        def _(dve):
            def split_weight(i):
                w, c = half_weight(i)
                dve.wait_ge(w_hi_ready, i + 1)
                nc.vector.tensor_tensor(w_lo[:, w, c], stage[i % len(stage)], w_hi[:, w, c].bitcast(F32),
                                        ALU.subtract).then_inc(w_lo_ready, 1)

            def weight_vectors():
                dve.wait_ge(vectors_in, 16)
                for c in range(FT):
                    dve.wait_ge(stage_in[c // HALF], 16)
                    for v in range(2):
                        if c:
                            dve.wait_ge(v_cols_ready, 2 * c + v - 1)
                        nc.vector.tensor_tensor_reduce(
                            out=(scores, mask_add)[v][:].rearrange("p m n -> p (m n)"), in0=stage[c // HALF][:, c % HALF],
                            in1=v_rows[:, v], scale=1.0, scalar=0.0, op0=ALU.mult, op1=ALU.add,
                            accum_out=v_cols[:, v, c:c + 1]).then_inc(v_cols_ready, 1)
                dve.wait_ge(v_psum_ready, 1)
                nc.vector.tensor_copy(v_rows[:], X[:]).then_inc(v_ready, 1)

            weight_vectors()

            def add_mask(k):
                wait(dve, wh_ready, k.done(layers=L0, per=DOTS))
                wait(dve, a_loaded[k.stream], graph_turn(k, STREAMS))
                nc.vector.tensor_scalar(mask_add[:], a_raw[:, k.stream], 0.5, MASKED, ALU.is_le,
                                        ALU.mult).then_inc(mask_ready, 1)

            def finish(k):
                if k.layer in (1, 3):
                    free_act_out(dve, k)
                if k.layer == 1 and k.turn is None:
                    dve.wait_ge(bias_in, 16)
                for n in range(NT):
                    here, psum, state = act_out[:, k.odd, n], O[:, k.odd, n], xs[:, k.stream, n]
                    if k.layer != 2:
                        wait(dve, o_ready, k.done(per=NT, part=n))
                    if k.layer == 0:
                        wait(dve, exp_out_ready, k.done(layers=L0, per=NT, part=n))
                        nc.vector.scalar_tensor_tensor(state, psum, 0.0, x_in[:, k.g0 % 2, n], ALU.max,
                                                       ALU.add).then_inc(dve_finished, 1)
                    if k.layer == 1:
                        nc.vector.scalar_tensor_tensor(here, psum, deg_rsqrt[:, k.stream, n:n + 1], bias_rows[:],
                                                       ALU.mult, ALU.add).then_inc(affine_ready, 1)
                    if k.layer == 2:
                        wait(dve, relu_ready, k.done(layers=L2, per=NT, part=n))
                        nc.vector.tensor_tensor(state, here, state, ALU.add).then_inc(dve_finished, 1)
                    if k.layer == 3:
                        nc.vector.scalar_tensor_tensor(here, psum, 0.0, state, ALU.max, ALU.add).then_inc(dve_finished, 1)
                if k.layer == 1:
                    for n in range(NT):
                        wait(dve, affine_ready, k.done(layers=L1, per=NT, part=n))
                        nc.vector.scalar_tensor_tensor(xs[:, k.stream, n], act_out[:, k.odd, n], 0.0,
                                                       xs[:, k.stream, n], ALU.max, ALU.add).then_inc(dve_finished, 1)

            def mask_scores(k):
                wait(dve, mask_ready, k.done(layers=L0))
                wait(dve, wh_rows_ready, k.done(layers=L0))
                for m in range(NT):
                    nc.vector.scalar_tensor_tensor(scores[:, m], wh_rows, wh[:, k.g0 % 2, 1, m:m + 1], mask_add[:, m],
                                                   ALU.add, ALU.add).then_inc(scores_ready, 1)
                wait(dve, scores_ready, k.done(layers=L0, per=NT))
                nc.vector.scalar_tensor_tensor(scores[:], scores[:], SLOPE, scores[:], ALU.mult,
                                               ALU.max).then_inc(masked_ready, 1)
                wait(dve, masked_ready, k.done(layers=L0))
                nc.vector.tensor_reduce(s_neg[:], scores[:], AX.X, ALU.max, negate=True).then_inc(neg_ready, 1)

            def softmax_parts(k):
                wait(dve, exp_ready, k.done(layers=L0, per=NT))
                nc.vector.reciprocal(s_rec[:], s_sum[:]).then_inc(s_rec_ready, 1)
                wait(dve, s_rec_ready, k.done(layers=L0))
                wait(dve, t_ready, k.done_by_last(0, per=2))
                for m in range(NT):
                    nc.vector.tensor_scalar(p_hi[:, m], scores[:, m], s_rec[:, m:m + 1], None,
                                            ALU.mult).then_inc(p_hi_ready, 1)
                for m in range(NT):
                    wait(dve, p_hi_ready, k.done(layers=L0, per=NT, part=m))
                    nc.vector.scalar_tensor_tensor(p_lo[:, m], scores[:, m], s_rec[:, m:m + 1],
                                                   p_hi[:, m].bitcast(F32), ALU.mult, ALU.subtract).then_inc(p_lo_ready, 1)

            def gather(k):
                if k.layer == 3:
                    transposed(k, 0)
                    wait(dve, recip_rows_ready, k.done(layers=L3))
                    wait(dve, mean_lo_ready, k.done(1, layers=L3, per=2))
                    for b in range(2):
                        c = slice(HALF * b, HALF * b + HALF)
                        wait(dve, t_ready, k.done(per=2, part=b))
                        nc.vector.tensor_tensor(t_mean[:, c], T[:, c], recip_rows[:].unsqueeze(1).to_broadcast([P, HALF, N]),
                                                ALU.mult).then_inc(t_mean_ready, 1)
                for b in range(2):
                    c = slice(HALF * b, HALF * b + HALF)
                    whole = t_mean if k.layer == 3 else T
                    wait(dve, t_hi_ready, k.done(per=2, part=b))
                    nc.vector.tensor_tensor(t_lo[:, k.odd, c], whole[:, c], t_hi[:, k.odd, c].bitcast(F32),
                                            ALU.subtract).then_inc(mean_lo_ready if k.layer == 3 else t_lo_ready, 1)

            def transposed(k, half):
                c = slice(HALF * half, HALF * half + HALF)
                wait(dve, ht_hi_ready, k.done(layers=L3, per=2, part=half))
                nc.vector.tensor_tensor(ht_lo[:, c], X[:, 1 - half].rearrange("p (f n) -> p f n", f=HALF),
                                        ht_hi[:, c].bitcast(F32), ALU.subtract).then_inc(ht_lo_ready, 1)

            def degrees(k):
                wait(dve, rows_loaded, k.affine(lambda i: 16 * (plan.graph(i) + 1)))
                nc.vector.tensor_reduce(deg[:, k.stream], a_rows[:], AX.X, ALU.add).then_inc(deg_ready, 1)
                wait(dve, deg_ready, k.done(layers=L0))
                nc.vector.tensor_scalar(deg_floor[:, k.stream], deg[:, k.stream], DEG_EPS, None,
                                        ALU.max).then_inc(deg_floor_ready, 1)
                wait(dve, deg_floor_ready, k.done(layers=L0))
                nc.vector.reciprocal(deg_recip[:, k.stream], deg_floor[:, k.stream]).then_inc(deg_recip_ready, 1)

            def statistics(k):
                if k.layer == 0:
                    source = x_in[:, k.g0 % 2]
                    wait(dve, x_loaded[k.g0 % 2], graph_turn(k, 2))
                else:
                    source = xs[:, k.stream]
                    if k.layer == 1:
                        wait(dve, elu_ready, k.done(4, layers=L0, per=NT))
                    else:
                        wait(dve, dve_finished, k.done(4, per=NT))
                wait(dve, ln_ready, k.done(2))
                for m in range(NT):
                    nc.vector.bn_stats(ln_stats[:, k.odd, m], source[:, m]).then_inc(stats_ready, 1)
                wait(dve, stats_ready, k.done(per=NT))
                nc.vector.memset(carrier[:], 0.0)
                for m in range(NT):
                    nc.vector.bn_aggr(ln_mv[:, k.odd, m], ln_stats[:, k.odd, m]).then_inc(mv_ready, 1)

            def prepare(k):
                if k.layer == 1:
                    diag, rest = flat_blocks(a_lo[:, k.stream])
                    hi_diag, hi_rest = flat_blocks(a_hi[:, k.stream].bitcast(F32))
                    raw_diag, raw_rest = flat_blocks(a_raw[:, k.stream])
                    wait(dve, ah_hi_ready, k.done(1, layers=L1, per=2))
                    nc.vector.tensor_tensor(a_diag[:], raw_diag, ident[:].unsqueeze(1).to_broadcast([P, NT, P]),
                                            ALU.add).then_inc(diag_ready, 1)
                    wait(dve, ah_hi_ready, k.done(layers=L1, per=2, part=0))
                    nc.vector.tensor_tensor(rest, raw_rest, hi_rest, ALU.subtract).then_inc(ah_lo_ready, 1)
                    wait(dve, ah_hi_ready, k.done(layers=L1, per=2, part=1))
                    nc.vector.tensor_tensor(diag, a_diag[:], hi_diag, ALU.subtract).then_inc(ah_lo_ready, 1)
                if k.layer == 2:
                    diag, _ = flat_blocks(a_lo[:, k.stream])
                    hi_diag, _ = flat_blocks(a_hi[:, k.stream].bitcast(F32))
                    raw_diag, _ = flat_blocks(a_raw[:, k.stream])
                    wait(dve, a_hi_ready, k.done(layers=L2))
                    nc.vector.tensor_tensor(diag, raw_diag, hi_diag, ALU.subtract).then_inc(a_lo_ready, 1)
                if k.layer == 0:
                    for m in range(NT):
                        wait(dve, h_ready, k.done(per=NT, part=m))
                        for v in range(2):
                            n = 2 * m + v
                            wait(dve, wh_ready, k.done(layers=L0, per=DOTS, part=n - 2) if n >= 2
                                 else k.done(1, layers=L0, per=DOTS))
                            nc.vector.tensor_tensor_reduce(
                                out=(scores, mask_add)[v][:].rearrange("p m n -> p (m n)"), in0=h[:, k.odd, m],
                                in1=v_rows[:, v], scale=1.0, scalar=0.0, op0=ALU.mult, op1=ALU.add,
                                accum_out=wh[:, k.g0 % 2, v, m:m + 1]).then_inc(wh_ready, 1)

            def mask_rows(k):
                wait(dve, h_ready, k.done(per=NT))
                nc.vector.tensor_scalar(row_mask[:, k.stream], h_sum[:, k.stream], 0.0, None,
                                        ALU.is_gt).then_inc(row_mask_ready, 1)

            for step in periods(dve):
                if step(3).layer == 0:
                    statistics(step(3))
                if step(2).layer == 0:
                    add_mask(step(2))
                if step(-1).valid:
                    finish(step(-1))
                if step(1).valid:
                    gather(step(1))
                if step(2).layer == 2:
                    mask_rows(step(2))
                if step(2).layer == 0:
                    mask_scores(step(2))
                    softmax_parts(step(2))
                if step(1).layer == 3:
                    transposed(step(1), 1)
                if step(2).layer == 0:
                    degrees(step(2))
                if step(3).layer in (1, 2, 3):
                    statistics(step(3))
                if step(3).valid:
                    prepare(step(3))
                if step.half is not None:
                    split_weight(step.half)

        @block.gpsimd
        def _(pool):
            nc.gpsimd.memset(ident[:], 0.0).then_inc(ident_zero, 1)
            for tile, value in ((minus_half, -0.5), (ones, 1.0), (ln_eps, LN_EPS), (minus_one, -1.0)):
                nc.gpsimd.memset(tile[:], value).then_inc(columns_ready, 1)
            pool.wait_ge(ident_zero, 1)
            nc.gpsimd.affine_select(out=ident[:], in_=ident[:], compare_op=ALU.not_equal, fill=1.0, base=0,
                                    pattern=[[-1, P]], channel_multiplier=1).then_inc(ident_ready, 1)
            pool.wait_ge(columns_ready, 4)

            def finish(k):
                if k.layer == 0:
                    for n in range(NT):
                        wait(pool, dve_finished, k.done(per=NT, part=n))
                        wait(pool, elu_neg_ready, k.done(layers=L0, per=NT, part=n))
                        nc.gpsimd.tensor_tensor(xs[:, k.stream, n], xs[:, k.stream, n], act_out[:, k.odd, n],
                                                ALU.subtract).then_inc(elu_ready, 1)

            def degrees(k):
                wait(pool, deg_ready, k.done(layers=L0))
                nc.gpsimd.tensor_tensor(deg_one[:, k.stream], deg[:, k.stream], ones[:], ALU.add).then_inc(deg_one_ready, 1)
                wait(pool, deg_one_ready, k.done(layers=L0))
                nc.gpsimd.tensor_tensor(deg_rsqrt[:, k.stream], deg_one[:, k.stream], minus_half[:],
                                        ALU.pow).then_inc(deg_rsqrt_ready, 1)

            def activate(k):
                b = k.odd
                wait(pool, h_ready, k.done(2, per=NT))
                wait(pool, h_hi_ready, k.done(2, per=NT))
                wait(pool, mv_ready, k.done(per=NT))
                nc.gpsimd.tensor_tensor(ln_var[:, b], ln_mv[:, b, :, 1], ln_eps[:], ALU.add).then_inc(ln_part, 1)
                wait(pool, ln_part, k.done(per=3, part=0))
                scale = ln_rstd[:, b] if k.layer == 1 else ln_scale[:, b]
                nc.gpsimd.tensor_tensor(scale, ln_var[:, b], minus_half[:], ALU.pow).then_inc(ln_part, 1)
                wait(pool, ln_part, k.done(per=3, part=1))
                if k.layer == 1:
                    wait(pool, deg_rsqrt_ready, k.done(layers=L0))
                    nc.gpsimd.tensor_tensor(ln_scale[:, b], ln_rstd[:, b], deg_rsqrt[:, k.stream],
                                            ALU.mult).then_inc(ln_scaled, 1)
                    wait(pool, ln_scaled, k.done(layers=L1))
                nc.gpsimd.tensor_tensor(ln_ms[:, b], ln_mv[:, b, :, 0], ln_scale[:, b], ALU.mult).then_inc(ln_part, 1)
                wait(pool, ln_part, k.done(per=3, part=2))
                nc.gpsimd.tensor_tensor(ln_bias[:, b], ln_ms[:, b], minus_one[:], ALU.mult).then_inc(ln_ready, 1)
                for m in range(NT):
                    wait(pool, h_ready, k.done(per=NT, part=m))
                    wait(pool, h_hi_ready, k.done(per=NT, part=m))
                    wait(pool, t_ready, k.done(2, per=2))
                    nc.gpsimd.tensor_tensor(h_lo[:, b, m], h[:, b, m], h_hi[:, b, m].bitcast(F32),
                                            ALU.subtract).then_inc(h_lo_ready, 1)

            for step in periods(pool):
                if step(2).layer in (1, 2, 3):
                    activate(step(2))
                if step(-1).valid:
                    finish(step(-1))
                if step(3).layer == 0:
                    activate(step(3))
                if step(2).layer == 0:
                    degrees(step(2))


def kernel(x, adj, L0_gnn_W, L0_gnn_a, L1_gnn_kernel, L1_gnn_bias, L2_gnn_kernel, L3_gnn_W):
    import numpy as np
    import concourse.bacc as bacc
    from concourse.bass_utils import run_bass_kernel_spmd

    x, adj = np.asarray(x), np.asarray(adj)
    w3_t = np.asarray(L3_gnn_W).T
    f = x.shape[-1]
    arrays = {
        "x": np.ascontiguousarray(x),
        "adj": np.ascontiguousarray(adj),
        "adj_t": np.ascontiguousarray(adj.transpose(0, 2, 1)),
        "w_all": np.ascontiguousarray(np.stack([np.asarray(L0_gnn_W), np.asarray(L1_gnn_kernel),
                                                np.asarray(L2_gnn_kernel), w3_t[:f], w3_t[f:]])),
        "a_vecs": np.ascontiguousarray(np.asarray(L0_gnn_a).reshape(2, f)),
        "bias": np.ascontiguousarray(np.asarray(L1_gnn_bias)),
    }
    nc = bacc.Bacc("TRN2", target_bir_lowering=False, num_devices=1)
    aps = {n: nc.dram_tensor(n, a.shape, F32, kind="ExternalInput").ap() for n, a in arrays.items()}
    out = nc.dram_tensor("out", x.shape, F32, kind="ExternalOutput").ap()
    gnn_kernel(nc, out=out, **aps)
    r = run_bass_kernel_spmd(nc, [arrays], core_ids=[0])
    return r.results[0]["out"]
```

```python
from contextlib import ExitStack

import concourse.bass as bass
from concourse import mybir

F32 = mybir.dt.float32
F32R = mybir.dt.float32r
ALU = mybir.AluOpType
ACT = mybir.ActivationFunctionType
AX = mybir.AxisListType

P = 128
LAYERS = 4
STREAMS = 4
MASKED = -9000000000000000.0
SLOPE = 0.2
LN_EPS = 1e-5
DEG_EPS = 1e-6
WEIGHTS = 5


class Schedule:

    def __init__(self, graphs):
        self.graphs = graphs
        self.turns = graphs // STREAMS
        self.rounds = LAYERS * self.turns + STREAMS - 1
        self.steps = STREAMS * self.rounds
        self.span = STREAMS * LAYERS
        self.first, self.last = -3, self.steps
        self.loop_at = self.span + STREAMS + 1
        whole = next(k for k in range(self.span, self.steps) if not self.valid(k))
        self.loops = (whole - 3 - self.loop_at) // self.span

    @staticmethod
    def late(stream):
        return -stream % STREAMS

    def valid(self, k):
        s, r = k % STREAMS, k // STREAMS
        return 0 <= k < self.steps and 0 <= r - self.late(s) < LAYERS * self.turns

    def layer(self, k):
        return (k // STREAMS + k % STREAMS) % LAYERS if self.valid(k) else None

    def graph(self, k):
        s, r = k % STREAMS, k // STREAMS
        return STREAMS * ((r - self.late(s)) // LAYERS) + self.late(s)

    def count(self, k, layers=range(LAYERS)):
        return sum(self.layer(i) in layers for i in range(k + 1) if self.valid(i))


class Step:

    def __init__(self, plan, k, turn):
        self.plan, self.k, self.turn = plan, k, turn
        self.valid, self.layer = plan.valid(k), plan.layer(k)
        self.stream = k % STREAMS
        self.odd = k % 2
        self.g0 = plan.graph(k) if self.valid else None

    def affine(self, value_at):
        base = value_at(self.k)
        if self.turn is None:
            return base
        slope = value_at(self.k + self.plan.span) - base
        for i in range(self.plan.loops):
            assert value_at(self.k + i * self.plan.span) == base + slope * i
        assert base > 0 or slope == 0, "a wait below one in the loop's first turn"
        return base + slope * self.turn if slope else base

    def graph(self, ahead=0):
        g = self.g0 + ahead
        return g if self.turn is None else g + STREAMS * self.turn

    def done(self, back=0, layers=range(LAYERS), per=1, part=None):
        def value_at(k):
            k -= back
            if part is None:
                return per * self.plan.count(k, layers)
            return per * self.plan.count(k - 1, layers) + (part + 1 if self.plan.layer(k) in layers else 0)
        return self.affine(value_at)

    def done_by_last(self, layer, per=1):
        def value_at(k):
            before = [i for i in range(k) if self.plan.layer(i) == layer]
            return per * self.plan.count(before[-1]) if before else 0
        return self.affine(value_at)


class Period:

    def __init__(self, plan, j, turn):
        self.plan, self.j, self.turn = plan, j, turn
        self.half = j + 3 if 0 <= j + 3 < 2 * WEIGHTS else None

    def __call__(self, n):
        return Step(self.plan, self.j + n, self.turn)


def gnn_kernel(nc, x, adj, adj_t, w_all, a_vecs, bias, out):
    G, N, F = x.shape
    NT = N // P
    FT = F // P
    HALF = FT // NT
    plan = Schedule(G)
    L0, L1, L2, L3, L012 = (0,), (1,), (2,), (3,), (0, 1, 2)
    DOTS = 2 * NT

    with ExitStack() as ctx:
        def sb(name, shape, dt=F32):
            return ctx.enter_context(nc.sbuf_tensor(name, shape, dt))

        def sem(name):
            return ctx.enter_context(nc.semaphore(name))

        w_hi = sb("w_hi", [P, WEIGHTS, FT, F], F32R)
        w_lo = sb("w_lo", [P, WEIGHTS, FT, F], F32R)
        v_rows = sb("v_rows", [P, 2, F])
        bias_rows = sb("bias_rows", [P, F])
        ident = sb("ident", [P, P])
        minus_half = sb("minus_half", [P, NT])
        carrier = sb("carrier", [P, 1])
        v_cols = sb("v_cols", [P, 2, FT])
        xs = sb("xs", [P, STREAMS, NT, F])
        a_raw = sb("a_raw", [P, STREAMS, NT, N])
        a_hi = sb("a_hi", [P, STREAMS, NT, N], F32R)
        a_lo = sb("a_lo", [P, STREAMS, NT, N], F32R)
        deg = sb("deg", [P, STREAMS, NT])
        deg_one = sb("deg_one", [P, STREAMS, NT])
        deg_rsqrt = sb("deg_rsqrt", [P, STREAMS, NT])
        deg_floor = sb("deg_floor", [P, STREAMS, NT])
        deg_recip = sb("deg_recip", [P, STREAMS, NT])
        x_in = sb("x_in", [P, 2, NT, F])
        a_rows = sb("a_rows", [P, NT, N])
        a_diag = sb("a_diag", [P, NT, P])
        h = sb("h", [P, 2, NT, F])
        h_hi = sb("h_hi", [P, 2, NT, F], F32R)
        h_lo = sb("h_lo", [P, 2, NT, F], F32R)
        t_hi = sb("t_hi", [P, 2, FT, N], F32R)
        t_lo = sb("t_lo", [P, 2, FT, N], F32R)
        t_mean = sb("t_mean", [P, FT, N])
        ht_hi = sb("ht_hi", [P, FT, N], F32R)
        ht_lo = sb("ht_lo", [P, FT, N], F32R)
        recip_rows = sb("recip_rows", [P, N])
        act_out = sb("act_out", [P, 2, NT, F])
        scores = sb("scores", [P, NT, N])
        mask_add = sb("mask_add", [P, NT, N])
        p_hi = sb("p_hi", [P, NT, N], F32R)
        p_lo = sb("p_lo", [P, NT, N], F32R)
        ln_stats = sb("ln_stats", [P, 2, NT, 6])
        ln_mv = sb("ln_mv", [P, 2, NT, 2])
        ln_var = sb("ln_var", [P, 2, NT])
        ln_rstd = sb("ln_rstd", [P, 2, NT])
        ln_scale = sb("ln_scale", [P, 2, NT])
        ln_neg_mean = sb("ln_neg_mean", [P, 2, NT])
        ln_bias = sb("ln_bias", [P, 2, NT])
        h_sum = sb("h_sum", [P, STREAMS, NT])
        row_mask = sb("row_mask", [P, STREAMS, NT])
        wh = sb("wh", [P, 2, 2, NT])
        s_neg = sb("s_neg", [P, NT])
        s_sum = sb("s_sum", [P, NT])
        s_rec = sb("s_rec", [P, NT])

        T = ctx.enter_context(nc.psum_tensor("T", [P, FT, N], F32))
        O = ctx.enter_context(nc.psum_tensor("O", [P, 2, NT, F], F32))
        X = ctx.enter_context(nc.psum_tensor("X", [P, 2, F], F32))
        wh_rows = X[:, 0, 0:N]
        recip_psum = X[:, 0, 0:N]

        stage = [xs[:, 1], xs[:, 2], t_mean[:].rearrange("p (c f) n -> p c (f n)", c=HALF)]

        def half_weight(i):
            return i // 2, slice(HALF * (i % 2), HALF * (i % 2) + HALF)

        stage_in = [sem(f"stage_in{b}") for b in range(len(stage))]
        vectors_in, bias_in = sem("vectors_in"), sem("bias_in")
        x_loaded = [sem(f"x_loaded{b}") for b in range(2)]
        a_loaded = [sem(f"a_loaded{s}") for s in range(STREAMS)]
        rows_loaded = sem("rows_loaded")
        out_stored = [sem(f"out_stored{b}") for b in range(2)]
        w_hi_ready, w_lo_ready = sem("w_hi_ready"), sem("w_lo_ready")
        v_cols_ready, v_psum_ready, v_ready = sem("v_cols_ready"), sem("v_psum_ready"), sem("v_ready")
        ident_zero, ident_ready, minus_half_ready = sem("ident_zero"), sem("ident_ready"), sem("minus_half_ready")
        t_ready, o_ready = sem("t_ready"), sem("o_ready")
        wh_rows_ready, recip_psum_ready, ht_psum_ready = sem("wh_rows_ready"), sem("recip_psum_ready"), sem("ht_psum_ready")
        stats_ready, mv_ready, ln_parts_ready, ln_rstd_ready, ln_scale_ready, ln_ready = (
            sem("stats_ready"), sem("mv_ready"), sem("ln_parts_ready"), sem("ln_rstd_ready"), sem("ln_scale_ready"),
            sem("ln_ready"))
        h_ready, h_hi_ready, h_lo_ready, row_mask_ready = (
            sem("h_ready"), sem("h_hi_ready"), sem("h_lo_ready"), sem("row_mask_ready"))
        deg_ready, deg_one_ready, deg_rsqrt_ready, deg_floor_ready, deg_recip_ready = (
            sem("deg_ready"), sem("deg_one_ready"), sem("deg_rsqrt_ready"), sem("deg_floor_ready"), sem("deg_recip_ready"))
        diag_ready, ah_hi_ready, ah_lo_ready, a_hi_ready, a_lo_ready = (
            sem("diag_ready"), sem("ah_hi_ready"), sem("ah_lo_ready"), sem("a_hi_ready"), sem("a_lo_ready"))
        wh_ready, mask_ready, scores_ready, masked_ready, neg_ready, exp_ready, s_rec_ready, p_hi_ready, p_lo_ready = (
            sem("wh_ready"), sem("mask_ready"), sem("scores_ready"), sem("masked_ready"), sem("neg_ready"),
            sem("exp_ready"), sem("s_rec_ready"), sem("p_hi_ready"), sem("p_lo_ready"))
        t_hi_ready, t_lo_ready, mean_lo_ready, t_mean_ready, recip_rows_ready, ht_hi_ready, ht_lo_ready = (
            sem("t_hi_ready"), sem("t_lo_ready"), sem("mean_lo_ready"), sem("t_mean_ready"), sem("recip_rows_ready"),
            sem("ht_hi_ready"), sem("ht_lo_ready"))
        exp_out_ready, elu_neg_ready, affine_ready, relu_ready, dve_finished, elu_ready = (
            sem("exp_out_ready"), sem("elu_neg_ready"), sem("affine_ready"), sem("relu_ready"),
            sem("dve_finished"), sem("elu_ready"))

        def periods(eng):
            for j in range(plan.first, plan.loop_at):
                yield Period(plan, j, None)
            with eng.Fori(0, plan.loops) as turn:
                for j in range(plan.loop_at, plan.loop_at + plan.span):
                    yield Period(plan, j, turn)
            for j in range(plan.loop_at + plan.span * plan.loops, plan.last + 2):
                yield Period(plan, j, None)

        def wait(eng, semaphore, value):
            if isinstance(value, int) and value <= 0:
                return
            eng.wait_ge(semaphore, value)

        def tiles(dram, g):
            return dram[g].rearrange("(m p) f -> p m f", p=P)

        def graph_turn(step, every, ahead=0):
            return step.affine(lambda k: 16 * ((plan.graph(k) + ahead) // every + 1))

        def free_act_out(eng, k):
            wait(eng, elu_ready, k.done(2, layers=L0, per=NT))
            wait(eng, dve_finished, k.done(2, per=NT))
            wait(eng, out_stored[k.odd], k.affine(lambda i: 16 * sum(
                plan.layer(e) == 3 for e in range(i - 1) if e % 2 == i % 2)))

        block = ctx.enter_context(nc.Block())

        @block.sync
        def _(sp):
            def load_half(i):
                w, c = half_weight(i)
                b = i % len(stage)
                if i >= len(stage):
                    sp.wait_ge(w_lo_ready, i - len(stage) + 1)
                sp.dma_start(stage[b], w_all[w].rearrange("(c p) n -> p c n", p=P)[:, c]).then_inc(stage_in[b], 16)

            sp.dma_start(x_in[:, 0], tiles(x, 0)).then_inc(x_loaded[0], 16)
            sp.dma_start(v_rows[:].rearrange("p v n -> p (v n)"),
                         a_vecs.rearrange("v n -> (v n)").partition_broadcast(P)).then_inc(vectors_in, 16)
            load_half(0)
            load_half(1)
            sp.dma_start(a_raw[:, 0], tiles(adj_t, 0)).then_inc(a_loaded[0], 16)
            sp.dma_start(a_rows[:], tiles(adj, 0)).then_inc(rows_loaded, 16)
            sp.dma_start(bias_rows[:], bias.partition_broadcast(P)).then_inc(bias_in, 16)
            load_half(2)
            sp.dma_start(x_in[:, 1], tiles(x, 1)).then_inc(x_loaded[1], 16)
            for g in range(1, STREAMS):
                s = -g % STREAMS
                sp.dma_start(a_raw[:, s], tiles(adj_t, g)).then_inc(a_loaded[s], 16)

            for step in periods(sp):
                if step.half is not None and step.half > 2:
                    load_half(step.half)
                done = step(-1)
                if done.layer == 3:
                    sp.wait_ge(dve_finished, done.done(per=NT))
                    sp.dma_start(tiles(out, done.graph()), act_out[:, done.odd]).then_inc(out_stored[done.stream % 2], 16)
                if done.layer == 0 and done.g0 + 2 < G:
                    sp.wait_ge(dve_finished, done.done(per=NT))
                    sp.dma_start(x_in[:, done.stream % 2], tiles(x, done.graph(2))).then_inc(x_loaded[done.stream % 2], 16)
                att = step(2)
                if att.layer == 0 and att.g0 + 1 < G:
                    sp.wait_ge(deg_ready, att.done(layers=L0))
                    sp.dma_start(a_rows[:], tiles(adj, att.graph(1))).then_inc(rows_loaded, 16)
                pre = step(3)
                if pre.layer == 2 and pre.g0 + STREAMS < G:
                    sp.wait_ge(a_lo_ready, pre.done(layers=L2))
                    sp.dma_start(a_raw[:, pre.stream], tiles(adj_t, pre.graph(STREAMS))).then_inc(a_loaded[pre.stream], 16)
            for b in range(2):
                sp.wait_ge(out_stored[b], 16 * (G // 2))

        @block.tensor
        def _(pe):
            def product(psum, pairs, start=True, stop=True):
                last = None
                for n, (s_hi, s_lo, m_hi, m_lo) in enumerate(pairs):
                    for i, (s, m) in enumerate(((s_hi, m_hi), (s_hi, m_lo), (s_lo, m_hi))):
                        last = nc.tensor.matmul(psum, s, m, start=(start and n == 0 and i == 0),
                                                stop=(stop and n == len(pairs) - 1 and i == 2))
                return last

            pe.wait_ge(ident_ready, 1)
            pe.wait_ge(v_cols_ready, 2 * FT)
            for v in range(2):
                for c in range(FT):
                    last = nc.tensor.transpose(X[:, v, c * P:c * P + P], v_cols[:, v, c:c + 1].to_broadcast([P, P]), ident[:])
            last.then_inc(v_psum_ready, 1)
            pe.wait_ge(v_ready, 1)

            def transpose_h(k, half):
                if half == 1:
                    wait(pe, recip_rows_ready, k.done(-1, layers=L3))
                    wait(pe, scores_ready, k.done(-1, layers=L0, per=NT))
                for f in range(HALF * half, HALF * half + HALF):
                    for m in range(NT):
                        c = (f % HALF) * N + m * P
                        last = nc.tensor.transpose(X[:, 1 - half, c:c + P], h[:, k.odd, m, f * P:f * P + P], ident[:])
                last.then_inc(ht_psum_ready, 1)

            def gather(k):
                if k.layer == 3:
                    wait(pe, ht_lo_ready, k.done(1, layers=L3, per=2))
                    wait(pe, h_ready, k.done(per=NT))
                    transpose_h(k, 0)
                wait(pe, h_hi_ready, k.done(per=NT))
                if k.layer == 0:
                    wait(pe, p_lo_ready, k.done(layers=L0, per=NT))
                    m_hi, m_lo = p_hi, p_lo
                else:
                    m_hi, m_lo = a_hi[:, k.stream], a_lo[:, k.stream]
                if k.layer == 1:
                    wait(pe, ah_hi_ready, k.done(layers=L1, per=2))
                    wait(pe, ah_lo_ready, k.done(layers=L1, per=2))
                if k.layer == 2:
                    wait(pe, a_hi_ready, k.done(layers=L2))
                    wait(pe, a_lo_ready, k.done(layers=L2))
                for b in range(2):
                    wait(pe, t_lo_ready, k.done(1, layers=L012, per=2, part=b))
                    wait(pe, t_mean_ready, k.done(1, layers=L3, per=2, part=b))
                    for f in range(HALF * b, HALF * b + HALF):
                        c = slice(f * P, f * P + P)
                        for m in range(NT):
                            if f == 0:
                                wait(pe, h_lo_ready, k.done(per=NT, part=m))
                            last = product(T[:, f], [(h_hi[:, k.odd, m, c], h_lo[:, k.odd, m, c], m_hi[:, m],
                                                      m_lo[:, m])], start=m == 0, stop=m == NT - 1)
                    last.then_inc(t_ready, 1)

            def spread(k):
                wait(pe, scores_ready, k.done(1, layers=L0, per=NT))
                wait(pe, recip_rows_ready, k.done(1, layers=L3))
                wait(pe, ht_lo_ready, k.done(2, layers=L3, per=2))
                if k.layer == 0:
                    wait(pe, wh_ready, k.done(layers=L0, per=DOTS))
                    columns, rows, ready = wh[:, k.g0 % 2, 0], wh_rows, wh_rows_ready
                else:
                    wait(pe, deg_recip_ready, k.done(layers=L0))
                    columns, rows, ready = deg_recip[:, k.stream], recip_psum, recip_psum_ready
                for m in range(NT):
                    last = nc.tensor.transpose(rows[:, m * P:m * P + P], columns[:, m:m + 1].to_broadcast([P, P]), ident[:])
                last.then_inc(ready, 1)

            def project(k):
                w = {0: 0, 1: 1, 2: 2, 3: 4}[k.layer]
                if k.turn is None:
                    wait(pe, w_lo_ready, 2 * w + 2)
                for n in range(NT):
                    c = slice(n * P, n * P + P)
                    wait(pe, dve_finished, k.done(2, per=NT, part=n))
                    for b in range(2):
                        if n == 0:
                            wait(pe, t_hi_ready, k.done(per=2, part=b))
                            wait(pe, *((mean_lo_ready, k.done(layers=L3, per=2, part=b)) if k.layer == 3 else
                                       (t_lo_ready, k.done(layers=L012, per=2, part=b))))
                        parts = [(t_hi[:, k.odd, f, c], t_lo[:, k.odd, f, c], w_hi[:, w, f], w_lo[:, w, f])
                                 for f in range(HALF * b, HALF * b + HALF)]
                        last = product(O[:, k.odd, n], parts, start=b == 0, stop=b == 1 and k.layer != 3)
                    if k.layer == 3:
                        if n == 0:
                            wait(pe, ht_hi_ready, k.done(layers=L3, per=2))
                            wait(pe, ht_lo_ready, k.done(layers=L3, per=2))
                        parts = [(ht_hi[:, f, c], ht_lo[:, f, c], w_hi[:, 3, f], w_lo[:, 3, f]) for f in range(FT)]
                        last = product(O[:, k.odd, n], parts, start=False)
                    last.then_inc(o_ready, 1)

            for step in periods(pe):
                if step(2).layer in (0, 3):
                    spread(step(2))
                if step(1).valid:
                    gather(step(1))
                if step(0).valid:
                    project(step(0))
                if step(1).layer == 3:
                    transpose_h(step(1), 1)

        def flat_blocks(t):
            flat = t.rearrange("p m n -> p (m n)")
            diag = t.rearrange("p m (b c) -> p (m b) c", b=NT)[:, 0:NT * NT:NT + 1]
            return diag, flat[:, P:NT * N - P]

        @block.scalar
        def _(act):
            def split_weight(i):
                w, c = half_weight(i)
                b = i % len(stage)
                act.wait_ge(stage_in[b], 16 * (i // len(stage) + 1))
                nc.scalar.copy(w_hi[:, w, c], stage[b]).then_inc(w_hi_ready, 1)

            def spread_recip(k):
                wait(act, recip_psum_ready, k.done(layers=L3))
                wait(act, mean_lo_ready, k.done(1, layers=L3, per=2))
                nc.scalar.copy(recip_rows[:], recip_psum).then_inc(recip_rows_ready, 1)

            def finish(k):
                if k.layer == 0:
                    for n in range(NT):
                        wait(act, o_ready, k.done(per=NT, part=n))
                        if n == 0:
                            free_act_out(act, k)
                        nc.scalar.activation(act_out[:, k.odd, n], O[:, k.odd, n], ACT.Exp).then_inc(exp_out_ready, 1)
                    for n in range(NT):
                        wait(act, exp_out_ready, k.done(layers=L0, per=NT, part=n))
                        nc.scalar.activation(act_out[:, k.odd, n], act_out[:, k.odd, n], ACT.Relu, bias=1.0,
                                             scale=-1.0).then_inc(elu_neg_ready, 1)
                if k.layer == 2:
                    for n in range(NT):
                        wait(act, o_ready, k.done(per=NT, part=n))
                        if n == 0:
                            free_act_out(act, k)
                            wait(act, row_mask_ready, k.done(layers=L2))
                        nc.scalar.activation(act_out[:, k.odd, n], O[:, k.odd, n], ACT.Relu,
                                             scale=row_mask[:, k.stream, n:n + 1]).then_inc(relu_ready, 1)

            def gather(k):
                wait(act, o_ready, k.done(2, per=NT))
                if k.layer == 3:
                    wait(act, o_ready, k.done_by_last(3, per=NT))
                    transposed(k, 0)
                    for b in range(2):
                        wait(act, t_mean_ready, k.done(layers=L3, per=2, part=b))
                        c = slice(HALF * b, HALF * b + HALF)
                        nc.scalar.copy(t_hi[:, k.odd, c], t_mean[:, c]).then_inc(t_hi_ready, 1)
                    return
                for b in range(2):
                    wait(act, t_ready, k.done(per=2, part=b))
                    c = slice(HALF * b, HALF * b + HALF)
                    nc.scalar.copy(t_hi[:, k.odd, c], T[:, c]).then_inc(t_hi_ready, 1)

            def transposed(k, half):
                wait(act, ht_psum_ready, k.done(layers=L3, per=2, part=half))
                nc.scalar.copy(ht_hi[:, HALF * half:HALF * half + HALF],
                               X[:, 1 - half].rearrange("p (f n) -> p f n", f=HALF)).then_inc(ht_hi_ready, 1)

            def exps(k):
                wait(act, neg_ready, k.done(layers=L0))
                for m in range(NT):
                    nc.scalar.activation(scores[:, m], scores[:, m], ACT.Exp, bias=s_neg[:, m:m + 1],
                                         accum_out=s_sum[:, m:m + 1]).then_inc(exp_ready, 1)

            def prepare(k):
                if k.layer == 1:
                    diag, rest = flat_blocks(a_hi[:, k.stream])
                    _, raw_rest = flat_blocks(a_raw[:, k.stream])
                    wait(act, t_ready, k.done(8, per=2))
                    wait(act, a_loaded[k.stream], graph_turn(k, STREAMS))
                    nc.scalar.copy(rest, raw_rest).then_inc(ah_hi_ready, 1)
                    wait(act, diag_ready, k.done(layers=L1))
                    nc.scalar.copy(diag, a_diag[:]).then_inc(ah_hi_ready, 1)
                if k.layer == 2:
                    diag, _ = flat_blocks(a_hi[:, k.stream])
                    raw_diag, _ = flat_blocks(a_raw[:, k.stream])
                    wait(act, t_ready, k.done(4, per=2))
                    nc.scalar.copy(diag, raw_diag).then_inc(a_hi_ready, 1)

            def activate(k):
                wait(act, ln_ready, k.done())
                wait(act, h_lo_ready, k.done(2, per=NT))
                wait(act, wh_ready, k.done(2, layers=L0, per=DOTS))
                wait(act, ht_psum_ready, k.done(2, layers=L3, per=2))
                source = x_in[:, k.g0 % 2] if k.layer == 0 else xs[:, k.stream]
                for m in range(NT):
                    scale, shift = ln_scale[:, k.odd, m:m + 1], ln_bias[:, k.odd, m:m + 1]
                    total = h_sum[:, k.stream, m:m + 1] if k.layer == 2 else None
                    nc.scalar.activation(h[:, k.odd, m], source[:, m], ACT.Relu, bias=shift, scale=scale,
                                         accum_out=total).then_inc(h_ready, 1)

            for step in periods(act):
                if step(2).layer == 3:
                    spread_recip(step(2))
                if step(2).layer in (1, 2, 3):
                    activate(step(2))
                if step(-1).valid:
                    finish(step(-1))
                if step(2).layer == 0:
                    exps(step(2))
                if step(3).layer == 0:
                    activate(step(3))
                if step(1).valid:
                    gather(step(1))
                if step(1).layer == 3:
                    transposed(step(1), 1)
                if step(3).valid:
                    prepare(step(3))
                if step.half is not None:
                    split_weight(step.half)

        @block.vector
        def _(dve):
            def split_weight(i):
                w, c = half_weight(i)
                dve.wait_ge(w_hi_ready, i + 1)
                nc.vector.tensor_tensor(w_lo[:, w, c], stage[i % len(stage)], w_hi[:, w, c].bitcast(F32),
                                        ALU.subtract).then_inc(w_lo_ready, 1)

            def weight_vectors():
                dve.wait_ge(vectors_in, 16)
                for c in range(FT):
                    dve.wait_ge(stage_in[c // HALF], 16)
                    for v in range(2):
                        if c:
                            dve.wait_ge(v_cols_ready, 2 * c + v - 1)
                        nc.vector.tensor_tensor_reduce(
                            out=(scores, mask_add)[v][:].rearrange("p m n -> p (m n)"), in0=stage[c // HALF][:, c % HALF],
                            in1=v_rows[:, v], scale=1.0, scalar=0.0, op0=ALU.mult, op1=ALU.add,
                            accum_out=v_cols[:, v, c:c + 1]).then_inc(v_cols_ready, 1)
                dve.wait_ge(v_psum_ready, 1)
                nc.vector.tensor_copy(v_rows[:], X[:]).then_inc(v_ready, 1)
                dve.wait_ge(v_ready, 1)

            def high_part(k):
                wait(dve, t_ready, k.done(2, per=2))
                for m in range(NT):
                    wait(dve, h_ready, k.done(per=NT, part=m))
                    nc.vector.tensor_copy(h_hi[:, k.odd, m], h[:, k.odd, m]).then_inc(h_hi_ready, 1)

            def add_mask(k):
                wait(dve, wh_ready, k.done(layers=L0, per=DOTS))
                wait(dve, a_loaded[k.stream], graph_turn(k, STREAMS))
                nc.vector.tensor_scalar(mask_add[:], a_raw[:, k.stream], 0.5, MASKED, ALU.is_le,
                                        ALU.mult).then_inc(mask_ready, 1)

            def finish(k):
                if k.layer in (1, 3):
                    free_act_out(dve, k)
                if k.layer == 1 and k.turn is None:
                    dve.wait_ge(bias_in, 16)
                for n in range(NT):
                    here, psum, state = act_out[:, k.odd, n], O[:, k.odd, n], xs[:, k.stream, n]
                    if k.layer != 2:
                        wait(dve, o_ready, k.done(per=NT, part=n))
                    if k.layer == 0:
                        wait(dve, exp_out_ready, k.done(layers=L0, per=NT, part=n))
                        nc.vector.scalar_tensor_tensor(state, psum, 0.0, x_in[:, k.g0 % 2, n], ALU.max,
                                                       ALU.add).then_inc(dve_finished, 1)
                    if k.layer == 1:
                        nc.vector.scalar_tensor_tensor(here, psum, deg_rsqrt[:, k.stream, n:n + 1], bias_rows[:],
                                                       ALU.mult, ALU.add).then_inc(affine_ready, 1)
                    if k.layer == 2:
                        wait(dve, relu_ready, k.done(layers=L2, per=NT, part=n))
                        nc.vector.tensor_tensor(state, here, state, ALU.add).then_inc(dve_finished, 1)
                    if k.layer == 3:
                        nc.vector.scalar_tensor_tensor(here, psum, 0.0, state, ALU.max, ALU.add).then_inc(dve_finished, 1)
                if k.layer == 1:
                    for n in range(NT):
                        wait(dve, affine_ready, k.done(layers=L1, per=NT, part=n))
                        nc.vector.scalar_tensor_tensor(xs[:, k.stream, n], act_out[:, k.odd, n], 0.0,
                                                       xs[:, k.stream, n], ALU.max, ALU.add).then_inc(dve_finished, 1)

            def mask_scores(k):
                wait(dve, mask_ready, k.done(layers=L0))
                wait(dve, wh_rows_ready, k.done(layers=L0))
                for m in range(NT):
                    nc.vector.scalar_tensor_tensor(scores[:, m], wh_rows, wh[:, k.g0 % 2, 1, m:m + 1], mask_add[:, m],
                                                   ALU.add, ALU.add).then_inc(scores_ready, 1)
                wait(dve, scores_ready, k.done(layers=L0, per=NT))
                nc.vector.scalar_tensor_tensor(scores[:], scores[:], SLOPE, scores[:], ALU.mult,
                                               ALU.max).then_inc(masked_ready, 1)
                wait(dve, masked_ready, k.done(layers=L0))
                nc.vector.tensor_reduce(s_neg[:], scores[:], AX.X, ALU.max, negate=True).then_inc(neg_ready, 1)

            def softmax_parts(k):
                wait(dve, exp_ready, k.done(layers=L0, per=NT))
                nc.vector.reciprocal(s_rec[:], s_sum[:]).then_inc(s_rec_ready, 1)
                wait(dve, s_rec_ready, k.done(layers=L0))
                wait(dve, t_ready, k.done_by_last(0, per=2))
                for m in range(NT):
                    nc.vector.tensor_scalar(p_hi[:, m], scores[:, m], s_rec[:, m:m + 1], None,
                                            ALU.mult).then_inc(p_hi_ready, 1)
                for m in range(NT):
                    wait(dve, p_hi_ready, k.done(layers=L0, per=NT, part=m))
                    nc.vector.scalar_tensor_tensor(p_lo[:, m], scores[:, m], s_rec[:, m:m + 1],
                                                   p_hi[:, m].bitcast(F32), ALU.mult, ALU.subtract).then_inc(p_lo_ready, 1)

            def gather(k):
                if k.layer == 3:
                    wait(dve, recip_rows_ready, k.done(layers=L3))
                    wait(dve, mean_lo_ready, k.done(1, layers=L3, per=2))
                    for b in range(2):
                        c = slice(HALF * b, HALF * b + HALF)
                        wait(dve, t_ready, k.done(per=2, part=b))
                        nc.vector.tensor_tensor(t_mean[:, c], T[:, c], recip_rows[:].unsqueeze(1).to_broadcast([P, HALF, N]),
                                                ALU.mult).then_inc(t_mean_ready, 1)
                for b in range(2):
                    c = slice(HALF * b, HALF * b + HALF)
                    whole = t_mean if k.layer == 3 else T
                    wait(dve, t_hi_ready, k.done(per=2, part=b))
                    nc.vector.tensor_tensor(t_lo[:, k.odd, c], whole[:, c], t_hi[:, k.odd, c].bitcast(F32),
                                            ALU.subtract).then_inc(mean_lo_ready if k.layer == 3 else t_lo_ready, 1)
                if k.layer == 3:
                    transposed(k, 0)

            def transposed(k, half):
                c = slice(HALF * half, HALF * half + HALF)
                wait(dve, ht_hi_ready, k.done(layers=L3, per=2, part=half))
                nc.vector.tensor_tensor(ht_lo[:, c], X[:, 1 - half].rearrange("p (f n) -> p f n", f=HALF),
                                        ht_hi[:, c].bitcast(F32), ALU.subtract).then_inc(ht_lo_ready, 1)

            def degrees(k):
                wait(dve, rows_loaded, k.affine(lambda i: 16 * (plan.graph(i) + 1)))
                nc.vector.tensor_reduce(deg[:, k.stream], a_rows[:], AX.X, ALU.add).then_inc(deg_ready, 1)
                wait(dve, deg_ready, k.done(layers=L0))
                nc.vector.tensor_scalar(deg_floor[:, k.stream], deg[:, k.stream], DEG_EPS, None,
                                        ALU.max).then_inc(deg_floor_ready, 1)
                nc.vector.tensor_scalar(deg_one[:, k.stream], deg[:, k.stream], 1.0, None,
                                        ALU.add).then_inc(deg_one_ready, 1)
                wait(dve, deg_floor_ready, k.done(layers=L0))
                nc.vector.reciprocal(deg_recip[:, k.stream], deg_floor[:, k.stream]).then_inc(deg_recip_ready, 1)

            def statistics(k):
                if k.layer == 0:
                    source = x_in[:, k.g0 % 2]
                    wait(dve, x_loaded[k.g0 % 2], graph_turn(k, 2))
                else:
                    source = xs[:, k.stream]
                for m in range(NT):
                    if k.layer == 1:
                        wait(dve, elu_ready, k.done(4, layers=L0, per=NT, part=m))
                    elif k.layer > 1:
                        wait(dve, dve_finished, k.done(4, per=NT, part=m))
                    nc.vector.bn_stats(ln_stats[:, k.odd, m], source[:, m]).then_inc(stats_ready, 1)
                wait(dve, stats_ready, k.done(per=NT))
                nc.vector.memset(carrier[:], 0.0)
                for m in range(NT):
                    nc.vector.bn_aggr(ln_mv[:, k.odd, m], ln_stats[:, k.odd, m]).then_inc(mv_ready, 1)
                wait(dve, mv_ready, k.done(per=NT))
                nc.vector.tensor_scalar(ln_var[:, k.odd], ln_mv[:, k.odd, :, 1], LN_EPS, None,
                                        ALU.add).then_inc(ln_parts_ready, 1)
                nc.vector.tensor_scalar(ln_neg_mean[:, k.odd], ln_mv[:, k.odd, :, 0], -1.0, None,
                                        ALU.mult).then_inc(ln_parts_ready, 1)

            def prepare(k):
                if k.layer == 1:
                    diag, rest = flat_blocks(a_lo[:, k.stream])
                    hi_diag, hi_rest = flat_blocks(a_hi[:, k.stream].bitcast(F32))
                    raw_diag, raw_rest = flat_blocks(a_raw[:, k.stream])
                    wait(dve, ah_hi_ready, k.done(1, layers=L1, per=2))
                    nc.vector.tensor_tensor(a_diag[:], raw_diag, ident[:].unsqueeze(1).to_broadcast([P, NT, P]),
                                            ALU.add).then_inc(diag_ready, 1)
                    wait(dve, ah_hi_ready, k.done(layers=L1, per=2, part=0))
                    nc.vector.tensor_tensor(rest, raw_rest, hi_rest, ALU.subtract).then_inc(ah_lo_ready, 1)
                    wait(dve, ah_hi_ready, k.done(layers=L1, per=2, part=1))
                    nc.vector.tensor_tensor(diag, a_diag[:], hi_diag, ALU.subtract).then_inc(ah_lo_ready, 1)
                if k.layer == 2:
                    diag, _ = flat_blocks(a_lo[:, k.stream])
                    hi_diag, _ = flat_blocks(a_hi[:, k.stream].bitcast(F32))
                    raw_diag, _ = flat_blocks(a_raw[:, k.stream])
                    wait(dve, a_hi_ready, k.done(layers=L2))
                    nc.vector.tensor_tensor(diag, raw_diag, hi_diag, ALU.subtract).then_inc(a_lo_ready, 1)
            def dots(k):
                for m in range(NT):
                    wait(dve, h_ready, k.done(per=NT, part=m))
                    for v in range(2):
                        n = 2 * m + v
                        wait(dve, wh_ready, k.done(layers=L0, per=DOTS, part=n - 2) if n >= 2
                             else k.done(1, layers=L0, per=DOTS))
                        nc.vector.tensor_tensor_reduce(
                            out=(scores, mask_add)[v][:].rearrange("p m n -> p (m n)"), in0=h[:, k.odd, m],
                            in1=v_rows[:, v], scale=1.0, scalar=0.0, op0=ALU.mult, op1=ALU.add,
                            accum_out=wh[:, k.g0 % 2, v, m:m + 1]).then_inc(wh_ready, 1)

            def mask_rows(k):
                wait(dve, h_ready, k.done(per=NT))
                nc.vector.tensor_scalar(row_mask[:, k.stream], h_sum[:, k.stream], 0.0, None,
                                        ALU.is_gt).then_inc(row_mask_ready, 1)

            for step in periods(dve):
                if step(2).layer == 0:
                    mask_scores(step(2))
                if step(3).layer == 0:
                    statistics(step(3))
                if step.j == plan.first:
                    weight_vectors()
                if step(2).layer in (1, 2, 3):
                    high_part(step(2))
                if step(-1).valid:
                    finish(step(-1))
                if step(3).layer in (2, 3):
                    statistics(step(3))
                if step(2).layer == 0:
                    softmax_parts(step(2))
                if step(3).layer == 0:
                    dots(step(3))
                if step(1).valid:
                    gather(step(1))
                if step(3).layer == 0:
                    high_part(step(3))
                    add_mask(step(3))
                if step(3).layer == 1:
                    statistics(step(3))
                if step(2).layer == 2:
                    mask_rows(step(2))
                if step(1).layer == 3:
                    transposed(step(1), 1)
                if step(2).layer == 0:
                    degrees(step(2))
                if step(3).valid:
                    prepare(step(3))
                if step.half is not None:
                    split_weight(step.half)

        @block.gpsimd
        def _(pool):
            nc.gpsimd.memset(ident[:], 0.0).then_inc(ident_zero, 1)
            nc.gpsimd.memset(minus_half[:], -0.5).then_inc(minus_half_ready, 1)
            pool.wait_ge(ident_zero, 1)
            nc.gpsimd.affine_select(out=ident[:], in_=ident[:], compare_op=ALU.not_equal, fill=1.0, base=0,
                                    pattern=[[-1, P]], channel_multiplier=1).then_inc(ident_ready, 1)
            pool.wait_ge(minus_half_ready, 1)

            def finish(k):
                if k.layer == 0:
                    for n in range(NT):
                        wait(pool, dve_finished, k.done(per=NT, part=n))
                        wait(pool, elu_neg_ready, k.done(layers=L0, per=NT, part=n))
                        nc.gpsimd.tensor_tensor(xs[:, k.stream, n], xs[:, k.stream, n], act_out[:, k.odd, n],
                                                ALU.subtract).then_inc(elu_ready, 1)

            def degrees(k):
                wait(pool, deg_one_ready, k.done(layers=L0))
                nc.gpsimd.tensor_tensor(deg_rsqrt[:, k.stream], deg_one[:, k.stream], minus_half[:],
                                        ALU.pow).then_inc(deg_rsqrt_ready, 1)

            def normalise(k):
                b = k.odd
                wait(pool, h_ready, k.done(2, per=NT))
                wait(pool, ln_parts_ready, k.done(per=2))
                rstd, rstd_ready = (ln_rstd, ln_rstd_ready) if k.layer == 1 else (ln_scale, ln_scale_ready)
                nc.gpsimd.tensor_tensor(rstd[:, b], ln_var[:, b], minus_half[:], ALU.pow).then_inc(rstd_ready, 1)
                if k.layer == 1:
                    wait(pool, deg_rsqrt_ready, k.done(4, layers=L0))
                    wait(pool, ln_rstd_ready, k.done(layers=L1))
                    nc.gpsimd.tensor_tensor(ln_scale[:, b], ln_rstd[:, b], deg_rsqrt[:, k.stream],
                                            ALU.mult).then_inc(ln_scale_ready, 1)
                wait(pool, ln_scale_ready, k.done())
                nc.gpsimd.tensor_tensor(ln_bias[:, b], ln_neg_mean[:, b], ln_scale[:, b], ALU.mult).then_inc(ln_ready, 1)

            def low_part(k):
                b = k.odd
                for m in range(NT):
                    wait(pool, h_ready, k.done(per=NT, part=m))
                    wait(pool, h_hi_ready, k.done(per=NT, part=m))
                    wait(pool, t_ready, k.done(2, per=2))
                    nc.gpsimd.tensor_tensor(h_lo[:, b, m], h[:, b, m], h_hi[:, b, m].bitcast(F32),
                                            ALU.subtract).then_inc(h_lo_ready, 1)

            for step in periods(pool):
                if step(3).layer == 0:
                    normalise(step(3))
                if step(2).layer in (1, 2, 3):
                    low_part(step(2))
                if step(-1).valid:
                    finish(step(-1))
                if step(3).layer in (1, 2, 3):
                    normalise(step(3))
                if step(3).layer == 0:
                    low_part(step(3))
                if step(2).layer == 0:
                    degrees(step(2))


def kernel(x, adj, L0_gnn_W, L0_gnn_a, L1_gnn_kernel, L1_gnn_bias, L2_gnn_kernel, L3_gnn_W):
    import numpy as np
    import concourse.bacc as bacc
    from concourse.bass_utils import run_bass_kernel_spmd

    x, adj = np.asarray(x), np.asarray(adj)
    w3_t = np.asarray(L3_gnn_W).T
    f = x.shape[-1]
    arrays = {
        "x": np.ascontiguousarray(x),
        "adj": np.ascontiguousarray(adj),
        "adj_t": np.ascontiguousarray(adj.transpose(0, 2, 1)),
        "w_all": np.ascontiguousarray(np.stack([np.asarray(L0_gnn_W), np.asarray(L1_gnn_kernel),
                                                np.asarray(L2_gnn_kernel), w3_t[:f], w3_t[f:]])),
        "a_vecs": np.ascontiguousarray(np.asarray(L0_gnn_a).reshape(2, f)),
        "bias": np.ascontiguousarray(np.asarray(L1_gnn_bias)),
    }
    nc = bacc.Bacc("TRN2", target_bir_lowering=False, num_devices=1)
    aps = {n: nc.dram_tensor(n, a.shape, F32, kind="ExternalInput").ap() for n, a in arrays.items()}
    out = nc.dram_tensor("out", x.shape, F32, kind="ExternalOutput").ap()
    gnn_kernel(nc, out=out, **aps)
    r = run_bass_kernel_spmd(nc, [arrays], core_ids=[0])
    return r.results[0]["out"]
```
